# Optimizing a Trainium2 kernel written in Bass

```python
import numpy as np
import jax
import jax.numpy as jnp

def _softmax(x, axis=-1):
    return jax.nn.softmax(x, axis=axis)

def _gelu(x):
    return jax.nn.gelu(x, approximate=True)

def _silu(x):
    return jax.nn.silu(x)

def _sigmoid(x):
    return jax.nn.sigmoid(x)

def _layernorm(x, axis=-1, eps=1e-05):
    m = jnp.mean(x, axis=axis, keepdims=True)
    v = jnp.var(x, axis=axis, keepdims=True)
    return (x - m) / jnp.sqrt(v + eps)

def _scatter_add(tgt, idx, src, axis=0):
    return tgt.at[idx].add(src)

def _segment_sum(src, seg, n):
    return jax.ops.segment_sum(src, seg, n)
kernel_name = 'mk_gnn_ffn_d1_gnn_r32_28f314'

def setup_inputs(seed: int=0):
    np.random.seed(seed)
    _w = jnp.asarray

    def _rec_inputs():
        import jax
        import jax.numpy as jnp
        _gk = jax.random.key(seed)
        x = -6.415e-05 + 1 * jax.random.normal(jax.random.fold_in(_gk, 1), (10000, 1024), jnp.float32)
        src = jax.random.randint(jax.random.fold_in(_gk, 2), (10000,), 0, 10000, jnp.int32)
        dst = jnp.minimum((10000 * jax.random.uniform(jax.random.fold_in(_gk, 3), (10000,)) ** 2.0).astype(jnp.int32), 9999)
        _o = jnp.argsort(dst, stable=True)
        src = src[_o]
        dst = dst[_o]
        return (x, src, dst)
    x, src, dst = _rec_inputs()

    def _L0_gnn_setup():
        import jax, jax.numpy as jnp
        import numpy as np
        NEG_SLOPE = 0.1
        EPS = 1e-05
        key = jax.random.key(seed)
        k1, k2, k3, k4, k5 = jax.random.split(key, 5)
        N, E, DIN, DOUT = (10000, 5000, 1024, 1024)
        x = jax.random.normal(k1, (N, DIN), dtype=jnp.float32)
        W = jax.random.normal(k2, (DIN, DOUT), dtype=jnp.float32) * 0.02
        a = jax.random.normal(k3, (1, 2 * DOUT), dtype=jnp.float32) * 0.02
        src = jax.random.randint(k4, (E,), 0, N, dtype=jnp.int64)
        dst = jax.random.randint(k5, (E,), 0, N, dtype=jnp.int64)
        return {'x': x, 'W': W, 'a': a, 'src': src, 'dst': dst}
    _L0_gnn_all = _L0_gnn_setup()
    _L0_gnn_in = {k: v for k, v in _L0_gnn_all.items() if k in ('W', 'a')}
    del _L0_gnn_all

    def _L0_ffn_setup():
        import jax, jax.numpy as jnp
        import numpy as np
        B, T, D, H = (4, 64, 1024, 64)
        E, S, K = (8, 2, 2)

        def _swiglu_stacked(x, w1, b1, w2, b2, w3, b3):
            p1 = jnp.einsum('btd,ndh->nbth', x, w1) + b1[:, None, None, :]
            p2 = jnp.einsum('btd,ndh->nbth', x, w2) + b2[:, None, None, :]
            glu = jax.nn.silu(p1) * p2
            return jnp.einsum('nbth,nhd->nbtd', glu, w3) + b3[:, None, None, :]
        key = jax.random.key(seed)
        ks = jax.random.split(key, 10)
        s = 0.02
        return {'x': jax.random.normal(ks[0], (B, T, D), jnp.float32), 'gate_w': jax.random.normal(ks[1], (D, E), jnp.float32) * s, 'gate_b': jnp.zeros((E,), jnp.float32), 'rw1': jax.random.normal(ks[2], (E, D, H), jnp.float32) * s, 'rb1': jnp.zeros((E, H), jnp.float32), 'rw2': jax.random.normal(ks[3], (E, D, H), jnp.float32) * s, 'rb2': jnp.zeros((E, H), jnp.float32), 'rw3': jax.random.normal(ks[4], (E, H, D), jnp.float32) * s, 'rb3': jnp.zeros((E, D), jnp.float32), 'sw1': jax.random.normal(ks[5], (S, D, H), jnp.float32) * s, 'sb1': jnp.zeros((S, H), jnp.float32), 'sw2': jax.random.normal(ks[6], (S, D, H), jnp.float32) * s, 'sb2': jnp.zeros((S, H), jnp.float32), 'sw3': jax.random.normal(ks[7], (S, H, D), jnp.float32) * s, 'sb3': jnp.zeros((S, D), jnp.float32)}
    _L0_ffn_all = _L0_ffn_setup()
    _L0_ffn_in = {k: v for k, v in _L0_ffn_all.items() if k in ('gate_w', 'gate_b', 'rw1', 'rb1', 'rw2', 'rb2', 'rw3', 'rb3', 'sw1', 'sb1', 'sw2', 'sb2', 'sw3', 'sb3')}
    del _L0_ffn_all
    return {'x': x, 'src': src, 'dst': dst, 'L0_gnn_W': _L0_gnn_in['W'], 'L0_gnn_a': _L0_gnn_in['a'], 'L0_ffn_gate_w': _L0_ffn_in['gate_w'], 'L0_ffn_gate_b': _L0_ffn_in['gate_b'], 'L0_ffn_rw1': _L0_ffn_in['rw1'], 'L0_ffn_rb1': _L0_ffn_in['rb1'], 'L0_ffn_rw2': _L0_ffn_in['rw2'], 'L0_ffn_rb2': _L0_ffn_in['rb2'], 'L0_ffn_rw3': _L0_ffn_in['rw3'], 'L0_ffn_rb3': _L0_ffn_in['rb3'], 'L0_ffn_sw1': _L0_ffn_in['sw1'], 'L0_ffn_sb1': _L0_ffn_in['sb1'], 'L0_ffn_sw2': _L0_ffn_in['sw2'], 'L0_ffn_sb2': _L0_ffn_in['sb2'], 'L0_ffn_sw3': _L0_ffn_in['sw3'], 'L0_ffn_sb3': _L0_ffn_in['sb3']}

def reference(x, src, dst, L0_gnn_W, L0_gnn_a, L0_ffn_gate_w, L0_ffn_gate_b, L0_ffn_rw1, L0_ffn_rb1, L0_ffn_rw2, L0_ffn_rb2, L0_ffn_rw3, L0_ffn_rb3, L0_ffn_sw1, L0_ffn_sb1, L0_ffn_sw2, L0_ffn_sb2, L0_ffn_sw3, L0_ffn_sb3):
    import jax
    import jax.numpy as jnp

    def _L0_gnn_ref(x, W, a, src, dst):
        import jax, jax.numpy as jnp
        import numpy as np
        NEG_SLOPE = 0.1
        EPS = 1e-05
        N = x.shape[0]
        d = W.shape[1]
        h = x @ W
        a_l, a_r = (a[0, :d], a[0, d:])
        al = h @ a_l
        ar = h @ a_r
        e = jnp.exp(-jax.nn.leaky_relu(al[src] + ar[dst], negative_slope=NEG_SLOPE))
        rowsum = jax.ops.segment_sum(e, src, num_segments=N)
        h_prime = jax.ops.segment_sum(e[:, None] * h[dst], src, num_segments=N)
        h_prime = h_prime / (rowsum[:, None] + EPS)
        return jax.nn.elu(h_prime)

    def _L0_ffn_ref(x, gate_w, gate_b, rw1, rb1, rw2, rb2, rw3, rb3, sw1, sb1, sw2, sb2, sw3, sb3):
        import jax, jax.numpy as jnp
        import numpy as np
        B, T, D, H = (4, 64, 1024, 64)
        E, S, K = (8, 2, 2)

        def _swiglu_stacked(x, w1, b1, w2, b2, w3, b3):
            p1 = jnp.einsum('btd,ndh->nbth', x, w1) + b1[:, None, None, :]
            p2 = jnp.einsum('btd,ndh->nbth', x, w2) + b2[:, None, None, :]
            glu = jax.nn.silu(p1) * p2
            return jnp.einsum('nbth,nhd->nbtd', glu, w3) + b3[:, None, None, :]
        scores = jax.nn.softmax(x @ gate_w + gate_b, axis=-1)
        weights, indices = jax.lax.top_k(scores, K)
        routed_all = _swiglu_stacked(x, rw1, rb1, rw2, rb2, rw3, rb3)
        out_bted = jnp.transpose(routed_all, (1, 2, 0, 3))
        gathered = jnp.take_along_axis(out_bted, indices[..., None], axis=2)
        routed = jnp.sum(weights[..., None] * gathered, axis=2)
        shared = _swiglu_stacked(x, sw1, sb1, sw2, sb2, sw3, sb3).mean(axis=0)
        return shared + routed
    x = x + _L0_gnn_ref(_layernorm(x, axis=-1), L0_gnn_W, L0_gnn_a, src, dst)
    x = x + _L0_ffn_ref(_layernorm(x, axis=-1)[None], L0_ffn_gate_w, L0_ffn_gate_b, L0_ffn_rw1, L0_ffn_rb1, L0_ffn_rw2, L0_ffn_rb2, L0_ffn_rw3, L0_ffn_rb3, L0_ffn_sw1, L0_ffn_sb1, L0_ffn_sw2, L0_ffn_sb2, L0_ffn_sw3, L0_ffn_sb3)[0]
    return x

_drawn_inputs = setup_inputs


def setup_inputs(seed=0):
    import zlib

    import numpy as np

    out = dict(_drawn_inputs(seed))
    spreads = {'L0_ffn_gate_b': (0.0, 0.688),
     'L0_ffn_rb1': (0.0, 0.8),
     'L0_ffn_rb2': (0.0, 0.8),
     'L0_ffn_rb3': (0.0, 0.475),
     'L0_ffn_sb1': (0.0, 2.0),
     'L0_ffn_sb2': (0.0, 2.0),
     'L0_ffn_sb3': (0.0, 0.312)}
    factors = {'L0_ffn_rw1': 5.024,
     'L0_ffn_rw2': 4.848,
     'L0_ffn_rw3': 4.795,
     'L0_ffn_sw1': 3.333,
     'L0_ffn_sw2': 3.9}
    for name, (base, spread) in spreads.items():
        noise = np.random.default_rng([zlib.crc32(name.encode()), seed]).standard_normal(out[name].shape)
        drawn = base * np.exp(spread * noise) if base else spread * noise
        out[name] = jnp.asarray(drawn.astype(out[name].dtype))
    for name, factor in factors.items():
        out[name] = (out[name] * factor).astype(out[name].dtype)
    return out
```

```python
import concourse.bass as bass
from concourse import mybir
from contextlib import ExitStack

N = 10000
E = 10000
D = 1024
NE, NS, H = 8, 2, 64
NX = NE + NS
G = NX * H
P = 128
KD = D // P
KG = G // P
UP = 2 * G + NE
CH = -(-E // P)
TL = -(-N // P)
ROW = D + 16
PAD_KEY = 16383
SKIP = 16384
ZW, ZR, ZN = 325, 50, 5
SLOPE = 0.1
EPS_ROW = 1e-5
EPS_LN = 1e-5
KB = 64
HALF = D // 2
EDGE_STEPS = 10
NODE_STEPS = 18


class Order:

    def __init__(self, eng, sem):
        self.eng, self.sem, self.base, self.n = eng, sem, 0, 0

    def done(self, instruction):
        instruction.then_inc(self.sem, 1)
        self.n += 1
        return instruction

    def wait(self):
        self.eng.wait_ge(self.sem, self.base + self.n)

    def enter(self, j, steps):
        self.before, self.steps = self.base + self.n, steps
        self.base, self.n = self.before + j * steps, 0

    def leave(self, turns):
        assert self.n == self.steps, (self.n, self.steps)
        self.base, self.n = self.before + turns * self.steps, 0


def build(nc, x, idx, keys, w, a, up, gate_b, b1, b2, dn, ob, out):
    f32, f32r, i32 = mybir.dt.float32, mybir.dt.float32r, mybir.dt.int32
    ALU = mybir.AluOpType
    ACT = mybir.ActivationFunctionType
    AX = mybir.AxisListType.X

    acc = nc.dram_tensor("acc", [N, ROW], f32).ap()
    w_rows = w.rearrange("(k p) n -> p k n", p=P)
    dn_rows = dn.rearrange("(k p) n -> p k n", p=P)

    whole, edges, nodes = ExitStack(), ExitStack(), ExitStack()
    with whole:
        def sem(name):
            return whole.enter_context(nc.semaphore(name))

        def tile(stack, name, shape, dt=f32):
            return stack.enter_context(nc.sbuf_tensor(name, shape, dt))

        def bank(stack, name, shape):
            return stack.enter_context(nc.psum_tensor(name, shape, f32))

        ident = tile(whole, "ident", [P, P])
        below = tile(whole, "below", [P, P])
        up_hi = tile(whole, "up_hi", [P, KD, UP], f32r)
        up_lo = tile(whole, "up_lo", [P, KD, UP], f32r)
        minus_half = tile(whole, "minus_half", [P, 2])
        stats = tile(whole, "stats", [P, 2, 12])
        mean_var = tile(whole, "mean_var", [P, 2, 2])
        var_eps = tile(whole, "var_eps", [P, 2])
        rstd = tile(whole, "rstd", [P, 2])
        affine = tile(whole, "affine", [P, 2])

        with edges:
            w_hi = tile(edges, "w_hi", [P, KD, D], f32r)
            w_lo = tile(edges, "w_lo", [P, KD, D], f32r)
            u_bc = tile(edges, "u_bc", [P, 2, D])
            u_sum = tile(edges, "u_sum", [P, 2])
            zeros = tile(edges, "zeros", [P, ZW])
            x_lo = tile(edges, "x_lo", [P, D], f32r)
            junk = x_lo
            result = tile(edges, "result", [P, 2, ROW])
            with ExitStack() as staging:
                w_raw = tile(staging, "w_raw", [P, 3, D])
                up_raw = tile(staging, "up_raw", [P, 2, UP])
                a_bc = tile(staging, "a_bc", [P, 2, D])
                u_col = tile(staging, "u_col", [P, 2, KD])
            src_rows = tile(edges, "src_rows", [P, 2, D])
            dst_rows = tile(edges, "dst_rows", [P, 2, D])
            x_hi = tile(edges, "x_hi", [P, D], f32r)
            same = tile(edges, "same", [P, P], f32r)
            aggT_hi = tile(edges, "aggT_hi", [P, 2, KD, P], f32r)
            aggT_lo = tile(edges, "aggT_lo", [P, 2, KD, P], f32r)
            edge_idx = [tile(edges, f"edge_idx{s}", [P, 3], i32) for s in range(2)]
            src_keys = tile(edges, "src_keys", [P, 2, P], i32)
            acc_idx = [tile(edges, f"acc_idx{s}", [P, 1], i32) for s in range(2)]
            src_key = tile(edges, "src_key", [P, 1])
            earlier = tile(edges, "earlier", [P, 1])
            dots = tile(edges, "dots", [P, 2])
            mean_u = tile(edges, "mean_u", [P, 2])
            logit = tile(edges, "logit", [P, 1])
            e_w = tile(edges, "e_w", [P, 1])
            acc_row = tile(edges, "acc_row", [P, 1])
            sum_row = tile(edges, "sum_row", [P, 2, 2])
            with ExitStack() as banks:
                agg = bank(banks, "agg", [P, D])
                hp = [bank(banks, f"hp{s}", [P, D]) for s in range(2)]
                e_sum = bank(banks, "e_sum", [P, HALF])

        with nodes:
            dn_hi = tile(nodes, "dn_hi", [P, KG, D], f32r)
            dn_lo = tile(nodes, "dn_lo", [P, KG, D], f32r)
            ob_raw = tile(nodes, "ob_raw", [KB, D])
            ob_hl = tile(nodes, "ob_hl", [KB, D], f32r)
            acc_t = tile(nodes, "acc_t", [P, 3, ROW])
            x1 = tile(nodes, "x1", [P, 3, D])
            out_t = tile(nodes, "out_t", [P, 3, D])
            exp_y = tile(nodes, "exp_y", [P, D])
            xn = tile(nodes, "xn", [P, D])
            xnT_hi = tile(nodes, "xnT_hi", [P, KD, P], f32r)
            xnT_lo = tile(nodes, "xnT_lo", [P, KD, P], f32r)
            p1 = tile(nodes, "p1", [P, G])
            p2 = tile(nodes, "p2", [P, G])
            th = tile(nodes, "th", [P, G])
            gT_hi = tile(nodes, "gT_hi", [P, KG, P], f32r)
            gT_lo = tile(nodes, "gT_lo", [P, KG, P], f32r)
            wT = tile(nodes, "wT", [KB, P], f32r)
            b1_bc = tile(nodes, "b1_bc", [P, G])
            b2_bc = tile(nodes, "b2_bc", [P, G])
            gb_bc = tile(nodes, "gb_bc", [P, NE])
            den = tile(nodes, "den", [P, 2])
            lg = tile(nodes, "lg", [P, NE])
            greater = tile(nodes, "greater", [P, NE, NE])
            equal = tile(nodes, "equal", [P, NE, NE])
            before = tile(nodes, "before", [P, NE, NE])
            rank = tile(nodes, "rank", [P, NE])
            neg_max = tile(nodes, "neg_max", [P, 1])
            exp_l = tile(nodes, "exp_l", [P, NE])
            exp_sum = tile(nodes, "exp_sum", [P, 2])
            x_w = tile(nodes, "x_w", [P, NX])
            x_w_hl = tile(nodes, "x_w_hl", [P, KB], f32r)
            with ExitStack() as banks:
                tp = bank(banks, "tp", [P, D])
                pu = bank(banks, "pu", [P, 3 * HALF])
                dp = bank(banks, "dp", [P, D])
                pg = bank(banks, "pg", [P, HALF])

        names = """const_ready a_loaded w_split u_cols u_ps u_bc_ready setup_done zero_ready
            split_ready agglo_ready agghi_ready agg_done wmm_done hp_free result_ready res_free
            acc_written var_ready rstd_ready logit_ready e_ready scale_ready xhi_ready
            dn_raw_free dnhi_ready dn_ready consts_loaded rinv_ready expy_ready norm_ready xn_ready
            t_done xhi_n xlo_n gate_done up_done pu_free p1_ready th_ready glu_ready v_done
            ghi_ready glo_ready d_done out_ready lmax_ready expl_ready mask_ready
            stats_done gathers_begun whi_ready uphi_ready up_split obhi_ready
            vector_step scalar_step pool_step""".split()
        S = {n: sem(n) for n in names}
        w_loaded = [sem(f"w_loaded{i}") for i in range(3)]
        up_loaded = [sem(f"up_loaded{i}") for i in range(2)]
        dn_loaded = [sem(f"dn_loaded{i}") for i in range(3)]
        idx_loaded = [sem(f"idx_loaded{i}") for i in range(2)]
        gathered = [sem(f"gathered{i}") for i in range(2)]
        tile_loaded = [sem(f"tile_loaded{i}") for i in range(3)]
        stored = [sem(f"stored{i}") for i in range(3)]
        block = whole.enter_context(nc.Block())

        def row0(t):
            return N - P if isinstance(t, int) and t == TL - 1 else t * P

        @block.sync
        def _(sp):
            sp.dma_start(a_bc[:, :, :], a.rearrange("o (l n) -> (o l) n", l=2).partition_broadcast(P)
                         ).then_inc(S["a_loaded"], 16)
            for k in range(KD):
                if k >= 3:
                    sp.wait_ge(S["w_split"], k - 2)
                sp.dma_start(w_raw[:, k % 3, :], w_rows[:, k, :]).then_inc(w_loaded[k % 3], 16)
            for k in range(KD):
                if k >= 2:
                    sp.wait_ge(S["up_split"], k - 1)
                sp.dma_start(up_raw[:, k % 2, :], up[:, k, :]).then_inc(up_loaded[k % 2], 16)

            def load_indices(k, s):
                sp.dma_start(edge_idx[s][:, :], idx[bass.ds(k * P, P), :]).then_inc(idx_loaded[s], 16)
                sp.dma_start(src_keys[:, s, :],
                             keys[bass.ds(k * P, P)].partition_broadcast(P)
                             ).then_inc(idx_loaded[s], 16)

            sp.wait_ge(S["setup_done"], 1)
            load_indices(0, 0)
            load_indices(1, 1)
            with sp.Fori(0, (CH - 3) // 2) as j:
                for s in range(2):
                    sp.wait_ge(S["split_ready"], j * 2 + s + 1)
                    load_indices(j * 2 + (s + 2), s)
            sp.wait_ge(S["split_ready"], CH - 2)
            load_indices(CH - 1, (CH - 1) % 2)

            def load_tile(t, j, u):
                sp.dma_start(x1[:, u, :], x[bass.ds(row0(t), P), :]).then_inc(tile_loaded[u], 16)
                sp.dma_start(acc_t[:, u, :], acc[bass.ds(row0(t), P), :]).then_inc(tile_loaded[u], 16)

            def store_tile(t, u):
                if isinstance(t, int) and t == TL - 1:
                    new = N - (TL - 1) * P
                    sp.dma_start(out[N - new:N, :], out_t[P - new:P, u, :]).then_inc(stored[u], 16)
                else:
                    sp.dma_start(out[bass.ds(row0(t), P), :], out_t[:, u, :]).then_inc(stored[u], 16)

            sp.wait_ge(S["acc_written"], 16 * (ZN + CH))
            for t in range(3):
                load_tile(t, 0, t)
            for k in range(KG):
                if k >= 3:
                    sp.wait_ge(S["dn_ready"], k - 2)
                sp.dma_start(out_t[:, k % 3, :], dn_rows[:, k, :]).then_inc(dn_loaded[k % 3], 16)
            sp.wait_ge(S["zero_ready"], 2)
            for r in (0, NX, 32, 32 + NX):
                sp.dma_start(ob_raw[r:r + NX, :], ob).then_inc(S["consts_loaded"], 16)
            sp.dma_start(b1_bc[:, :], b1.partition_broadcast(P)).then_inc(S["consts_loaded"], 16)
            sp.dma_start(b2_bc[:, :], b2.partition_broadcast(P)).then_inc(S["consts_loaded"], 16)
            sp.dma_start(gb_bc[:, :], gate_b.partition_broadcast(P)).then_inc(S["consts_loaded"], 16)
            with sp.Fori(0, (TL - 4) // 3) as j:
                for u in range(3):
                    sp.wait_ge(S["out_ready"], j * 3 + u + 1)
                    store_tile(j * 3 + u, u)
                    load_tile(j * 3 + (u + 3), j, u)
            for t in range(TL - 4, TL):
                sp.wait_ge(S["out_ready"], t + 1)
                store_tile(t, t % 3)
                if t + 3 < TL:
                    load_tile(t + 3, 0, t % 3)
            for u in range(3):
                sp.wait_ge(stored[u], 16 * len(range(u, TL, 3)))

        @block.gpsimd
        def _(pool):
            order = Order(pool, S["pool_step"])
            pool.memset(zeros[:, :], 0.0).then_inc(S["zero_ready"], 1)
            order.done(pool.memset(ident[:, :], 0.0))
            order.done(pool.memset(below[:, :], 1.0))
            pool.memset(minus_half[:, :], -0.5).then_inc(S["const_ready"], 1)
            order.wait()
            pool.affine_select(out=ident[:, :], in_=ident[:, :], compare_op=ALU.not_equal, fill=1.0,
                               base=0, pattern=[[-1, P]], channel_multiplier=1).then_inc(S["const_ready"], 1)
            pool.affine_select(out=below[:, :], in_=below[:, :], compare_op=ALU.is_gt, fill=0.0,
                               base=0, pattern=[[-1, P]], channel_multiplier=1).then_inc(S["const_ready"], 1)
            pool.wait_ge(S["zero_ready"], 1)
            flat = acc.rearrange("n r -> (n r)").rearrange("(p z r w) -> p z r w", p=P, z=ZN, r=ZR)
            for z in range(ZN):
                pool.dma_start(flat[:, z, :, :], zeros[:, :].unsqueeze(1).to_broadcast([P, ZR, ZW])
                               ).then_inc(S["acc_written"], 16)

            def gather(k, s, turn):
                pool.wait_ge(idx_loaded[s], 32 * (turn + 1))
                pool.sem_inc(S["gathers_begun"], 1)
                for rows, col in ((src_rows, 1), (dst_rows, 2)):
                    pool.indirect_dma_start(
                        out=rows[:, s, :], out_offset=None, in_=x,
                        in_offset=bass.IndirectOffsetOnAxis(ap=edge_idx[s][:, col:col + 1], axis=0)
                        ).then_inc(gathered[s], 16)

            def power(k):
                pool.wait_ge(S["var_ready"], k + 1)
                pool.tensor_tensor(out=rstd[:, :], in0=var_eps[:, :], in1=minus_half[:, :],
                                   op=ALU.pow).then_inc(S["rstd_ready"], 1)

            def scatter(k, s):
                pool.wait_ge(S["result_ready"], k + 1)
                pool.wait_ge(S["acc_written"], (k + ZN) * 16)
                pool.sem_inc(S["res_free"], 1)
                pool.indirect_dma_start(
                    out=acc, out_offset=bass.IndirectOffsetOnAxis(ap=acc_idx[s][:, :], axis=0),
                    in_=result[:, s, :], in_offset=None, bounds_check=N - 1, oob_is_err=False,
                    compute_op=ALU.add).then_inc(S["acc_written"], 16)

            pool.sem_inc(S["res_free"], 1)
            gather(0, 0, 0)
            gather(1, 1, 0)
            power(0)
            pool.wait_ge(S["split_ready"], 1)
            gather(2, 0, 1)
            power(1)
            with pool.Fori(0, (CH - 3) // 2) as j:
                for s in range(2):
                    pool.wait_ge(S["split_ready"], j * 2 + (s + 2))
                    gather(j * 2 + (s + 3), 1 - s, j + (s + 3) // 2)
                    power(j * 2 + (s + 2))
                    scatter(j * 2 + s, s)
            power(CH - 1)
            for k in range(CH - 3, CH):
                scatter(k, k % 2)

            pool.wait_ge(S["acc_written"], 16 * (ZN + CH))
            pool.memset(ob_raw[:, :], 0.0).then_inc(S["zero_ready"], 1)
            order.done(pool.memset(before[:, :, :], 1.0))
            order.wait()
            pool.affine_select(out=before[:, :, :], in_=before[:, :, :], compare_op=ALU.is_gt, fill=0.0,
                               base=0, pattern=[[1, NE], [-1, NE]], channel_multiplier=0
                               ).then_inc(S["const_ready"], 1)
            with pool.Fori(0, TL) as t:
                power(t + CH)

        @block.scalar
        def _(act):
            order = Order(act, S["scalar_step"])
            act.wait_ge(S["const_ready"], 3)
            for k in range(KD):
                act.wait_ge(w_loaded[k % 3], 16 * (k // 3 + 1))
                act.activation(w_hi[:, k, :], w_raw[:, k % 3, :], ACT.Copy).then_inc(S["whi_ready"], 1)
            for k in range(KD):
                act.wait_ge(up_loaded[k % 2], 16 * (k // 2 + 1))
                act.activation(up_hi[:, k, :], up_raw[:, k % 2, :], ACT.Copy).then_inc(S["uphi_ready"], 1)
            for l in range(2):
                act.wait_ge(S["u_ps"], l + 1)
                act.activation(u_bc[:, l, :], hp[l][:, :], ACT.Copy).then_inc(S["u_bc_ready"], 1)
            act.wait_ge(S["u_bc_ready"], 2)
            act.sem_inc(S["hp_free"], 2)

            def edge_rows(k, s):
                act.wait_ge(S["logit_ready"], k + 1)
                act.activation(e_w[:, :], logit[:, :], ACT.Exp, scale=-1.0).then_inc(S["e_ready"], 1)
                act.wait_ge(S["scale_ready"], k + 1)
                order.done(act.activation(dst_rows[:, s, :], dst_rows[:, s, :], ACT.Identity,
                                          scale=affine[:, 0:1], bias=affine[:, 1:2]))
                order.wait()
                act.activation(x_hi[:, :], dst_rows[:, s, :], ACT.Copy).then_inc(S["xhi_ready"], 1)

            def agg_hi(k, s):
                act.wait_ge(S["agg_done"], k + 1)
                act.activation(aggT_hi[:, s, :, :].rearrange("p k e -> p (k e)"), agg[:, :], ACT.Copy
                               ).then_inc(S["agghi_ready"], 1)

            def evacuate(k, s):
                act.wait_ge(S["wmm_done"], k + 1)
                act.wait_ge(S["res_free"], k + 1)
                act.activation(result[:, s, 0:D], hp[s][:, :], ACT.Copy).then_inc(S["hp_free"], 1)
                act.activation(result[:, s, D:D + 1], sum_row[:, s, 0:1], ACT.Copy)
                act.activation(acc_idx[s][:, :], sum_row[:, s, 1:2], ACT.Copy).then_inc(S["result_ready"], 1)

            for k in range(2):
                edge_rows(k, k)
                agg_hi(k, k)
            with act.Fori(0, (CH - 3) // 2) as j:
                order.enter(j, 2)
                for s in range(2):
                    edge_rows(j * 2 + (s + 2), s)
                    evacuate(j * 2 + s, s)
                    agg_hi(j * 2 + (s + 2), s)
            order.leave((CH - 3) // 2)
            edge_rows(CH - 1, 0)
            evacuate(CH - 3, 0)
            agg_hi(CH - 1, 0)
            evacuate(CH - 2, 1)
            evacuate(CH - 1, 0)

            def front(t, u):
                act.wait_ge(S["rinv_ready"], t + 1)
                act.activation(exp_y[:, :], acc_t[:, u, 0:D], ACT.Exp, scale=den[:, 1:2]
                               ).then_inc(S["expy_ready"], 1)
                act.wait_ge(S["norm_ready"], t + 1)
                act.activation(xn[:, :], x1[:, u, :], ACT.Identity, scale=affine[:, 0:1],
                               bias=affine[:, 1:2]).then_inc(S["xn_ready"], 1)

            def xnT(t):
                act.wait_ge(S["t_done"], t + 1)
                act.activation(xnT_hi[:, :, :].rearrange("p k e -> p (k e)"), tp[:, :], ACT.Copy
                               ).then_inc(S["xhi_n"], 1)

            def gT(t):
                act.wait_ge(S["v_done"], t + 1)
                act.activation(gT_hi[:, :, :].rearrange("p k e -> p (k e)"), tp[:, 0:G], ACT.Copy
                               ).then_inc(S["ghi_ready"], 1)

            def experts(t):
                act.wait_ge(S["lmax_ready"], t + 1)
                act.activation(exp_l[:, :], lg[:, :], ACT.Exp, bias=neg_max[:, :],
                               accum_out=exp_sum[:, 0:1]).then_inc(S["expl_ready"], 1)
                act.wait_ge(S["p1_ready"], t + 1)
                act.activation(th[:, :], p1[:, :], ACT.Tanh, scale=0.5).then_inc(S["th_ready"], 1)

            front(0, 0)
            xnT(0)
            for k in range(KG):
                act.wait_ge(dn_loaded[k % 3], 16 * (k // 3 + 1))
                act.activation(dn_hi[:, k, :], out_t[:, k % 3, :], ACT.Copy).then_inc(S["dnhi_ready"], 1)
            act.wait_ge(S["consts_loaded"], 16 * 7)
            act.activation(ob_hl[:, :], ob_raw[:, :], ACT.Copy, scale=2.0).then_inc(S["obhi_ready"], 1)

            def step(t, u):
                if not isinstance(t, int) or t > 0:
                    gT(t - 1)
                if not isinstance(t, int) or t < TL - 1:
                    front(t + 1, (u + 1) % 3)
                experts(t)
                if not isinstance(t, int) or t < TL - 1:
                    xnT(t + 1)

            step(0, 0)
            with act.Fori(0, (TL - 4) // 3) as j:
                for v in range(1, 4):
                    step(j * 3 + v, v % 3)
            for t in range(TL - 3, TL):
                step(t, t % 3)
            gT(TL - 1)

        @block.vector
        def _(dve):
            order = Order(dve, S["vector_step"])
            dve.memset(result[:, :, D:ROW], 0.0)
            dve.wait_ge(S["a_loaded"], 16)
            for k in range(KD):
                dve.wait_ge(w_loaded[k % 3], 16 * (k // 3 + 1))
                for l in range(2):
                    order.wait()
                    order.done(dve.tensor_tensor_reduce(
                        out=junk[:, :], in0=w_raw[:, k % 3, :], in1=a_bc[:, l, :], scale=1.0, scalar=0.0,
                        op0=ALU.mult, op1=ALU.add, accum_out=u_col[:, l, k:k + 1]))
                dve.wait_ge(S["whi_ready"], k + 1)
                dve.tensor_tensor(out=w_lo[:, k, :], in0=w_raw[:, k % 3, :],
                                  in1=w_hi[:, k, :].bitcast(f32), op=ALU.subtract).then_inc(S["w_split"], 1)
            for k in range(KD):
                dve.wait_ge(up_loaded[k % 2], 16 * (k // 2 + 1))
                dve.wait_ge(S["uphi_ready"], k + 1)
                dve.tensor_tensor(out=up_lo[:, k, :], in0=up_raw[:, k % 2, :],
                                  in1=up_hi[:, k, :].bitcast(f32), op=ALU.subtract).then_inc(S["up_split"], 1)
            dve.wait_ge(S["u_bc_ready"], 2)
            dve.tensor_reduce(out=u_sum[:, :], in_=u_bc[:, :, :], axis=AX, op=ALU.add
                              ).then_inc(S["setup_done"], 1)
            dve.wait_ge(S["setup_done"], 1)

            def edge_rows(k, s, turn):
                def dot(r):
                    order.done(dve.tensor_tensor_reduce(
                        out=junk[:, :], in0=(src_rows, dst_rows)[r][:, s, :], in1=u_bc[:, r, :],
                        scale=1.0, scalar=0.0, op0=ALU.mult, op1=ALU.add, accum_out=dots[:, r:r + 1]))

                dve.wait_ge(gathered[s], 32 * (turn + 1))
                for r, rows in enumerate((src_rows, dst_rows)):
                    for h in range(2):
                        last = dve.bn_stats(out=stats[:, r, 6 * h:6 * h + 6],
                                            in_=rows[:, s, h * HALF:(h + 1) * HALF])
                order.done(last)
                order.wait()
                dot(0)
                for r in range(2):
                    last = dve.bn_aggr(out=mean_var[:, r, :], in_=stats[:, r, :])
                order.done(last)
                order.wait()
                dve.tensor_scalar(out=var_eps[:, :], in0=mean_var[:, :, 1], scalar1=EPS_LN, scalar2=None,
                                  op0=ALU.add).then_inc(S["var_ready"], 1)
                dot(1)
                dve.tensor_tensor(out=mean_u[:, :], in0=mean_var[:, :, 0], in1=u_sum[:, :], op=ALU.mult)
                dve.wait_ge(idx_loaded[s], 32 * (turn + 1))
                order.done(dve.tensor_copy(src_key[:, :], edge_idx[s][:, 0:1]))
                order.wait()
                order.done(dve.tensor_tensor(out=dots[:, :], in0=dots[:, :], in1=mean_u[:, :], op=ALU.subtract))
                order.done(dve.tensor_scalar(out=same[:, :], in0=src_keys[:, s, :], scalar1=src_key[:, :],
                                             scalar2=None, op0=ALU.is_equal))
                order.wait()
                order.done(dve.tensor_tensor_reduce(out=junk[:, 0:P], in0=same[:, :].bitcast(f32), in1=below[:, :],
                                                    scale=1.0, scalar=0.0, op0=ALU.mult, op1=ALU.add,
                                                    accum_out=earlier[:, :]))
                dve.wait_ge(S["rstd_ready"], k + 1)
                order.done(dve.tensor_tensor_reduce(out=junk[:, P:P + 2], in0=dots[:, :], in1=rstd[:, :],
                                                    scale=1.0, scalar=0.0, op0=ALU.mult, op1=ALU.add,
                                                    accum_out=logit[:, :]))
                order.wait()
                dve.scalar_tensor_tensor(out=logit[:, :], in0=logit[:, :], scalar=SLOPE, in1=logit[:, :],
                                         op0=ALU.mult, op1=ALU.max).then_inc(S["logit_ready"], 1)
                dve.scalar_tensor_tensor(out=acc_row[:, :], in0=earlier[:, :], scalar=float(SKIP),
                                         in1=src_key[:, :], op0=ALU.mult, op1=ALU.add)
                dve.wait_ge(S["e_ready"], k + 1)
                order.done(dve.tensor_tensor(out=affine[:, 0:1], in0=e_w[:, :], in1=rstd[:, 1:2], op=ALU.mult))
                order.wait()
                dve.scalar_tensor_tensor(out=affine[:, 1:2], in0=mean_var[:, 1, 0:1], scalar=-1.0,
                                         in1=affine[:, 0:1], op0=ALU.mult, op1=ALU.mult
                                         ).then_inc(S["scale_ready"], 1)
                dve.wait_ge(S["xhi_ready"], k + 1)
                dve.tensor_tensor(out=x_lo[:, :], in0=dst_rows[:, s, :], in1=x_hi[:, :].bitcast(f32),
                                  op=ALU.subtract).then_inc(S["split_ready"], 1)

            def agg_lo(k, s):
                dve.wait_ge(S["agg_done"], k + 1)
                dve.wait_ge(S["agghi_ready"], k + 1)
                dve.tensor_copy(sum_row[:, s, 0:1], e_sum[:, 0:1])
                dve.tensor_copy(sum_row[:, s, 1:2], acc_row[:, :])
                dve.tensor_tensor(out=aggT_lo[:, s, :, :].rearrange("p k e -> p (k e)"), in0=agg[:, :],
                                  in1=aggT_hi[:, s, :, :].rearrange("p k e -> p (k e)").bitcast(f32),
                                  op=ALU.subtract).then_inc(S["agglo_ready"], 1)

            with dve.Fori(0, CH // 2) as j:
                order.enter(j, 2 * EDGE_STEPS)
                for s in range(2):
                    edge_rows(j * 2 + s, s, j)
                    agg_lo(j * 2 + s, s)
            order.leave(CH // 2)
            edge_rows(CH - 1, 0, CH // 2)
            agg_lo(CH - 1, 0)

            def front(t, u, turn):
                dve.wait_ge(tile_loaded[u], 32 * (turn + 1))
                order.done(dve.tensor_scalar(out=den[:, 0:1], in0=acc_t[:, u, D:D + 1], scalar1=EPS_ROW,
                                             scalar2=None, op0=ALU.add))
                order.wait()
                dve.reciprocal(den[:, 1:2], den[:, 0:1]).then_inc(S["rinv_ready"], 1)
                dve.wait_ge(S["expy_ready"], t + 1)
                order.done(dve.tensor_scalar(out=exp_y[:, :], in0=exp_y[:, :], scalar1=1.0, scalar2=-1.0,
                                             op0=ALU.min, op1=ALU.add))
                order.wait()
                order.done(dve.scalar_tensor_tensor(out=acc_t[:, u, 0:D], in0=acc_t[:, u, 0:D],
                                                    scalar=den[:, 1:2], in1=exp_y[:, :],
                                                    op0=ALU.mult, op1=ALU.max))
                order.wait()
                order.done(dve.tensor_tensor(out=x1[:, u, :], in0=x1[:, u, :], in1=acc_t[:, u, 0:D], op=ALU.add))
                order.wait()
                for h in range(2):
                    last = dve.bn_stats(out=stats[:, 0, 6 * h:6 * h + 6],
                                        in_=x1[:, u, h * HALF:(h + 1) * HALF])
                order.done(last)
                order.wait()
                dve.sem_inc(S["stats_done"], 1)
                order.done(dve.bn_aggr(out=mean_var[:, 0, :], in_=stats[:, 0, :]))
                order.wait()
                dve.tensor_scalar(out=var_eps[:, :], in0=mean_var[:, :, 1], scalar1=EPS_LN, scalar2=None,
                                  op0=ALU.add).then_inc(S["var_ready"], 1)
                dve.wait_ge(S["rstd_ready"], t + (CH + 1))
                dve.tensor_copy(affine[:, 0:1], rstd[:, 0:1])
                dve.scalar_tensor_tensor(out=affine[:, 1:2], in0=mean_var[:, 0, 0:1], scalar=-1.0,
                                         in1=rstd[:, 0:1], op0=ALU.mult, op1=ALU.mult
                                         ).then_inc(S["norm_ready"], 1)

            def xnT(t):
                dve.wait_ge(S["xhi_n"], t + 1)
                dve.tensor_tensor(out=xnT_lo[:, :, :].rearrange("p k e -> p (k e)"), in0=tp[:, :],
                                  in1=xnT_hi[:, :, :].rearrange("p k e -> p (k e)").bitcast(f32),
                                  op=ALU.subtract).then_inc(S["xlo_n"], 1)

            def gT(t):
                dve.wait_ge(S["ghi_ready"], t + 1)
                dve.tensor_copy(wT[:, :], tp[0:KB, G:G + P])
                dve.tensor_tensor(out=gT_lo[:, :, :].rearrange("p k e -> p (k e)"), in0=tp[:, 0:G],
                                  in1=gT_hi[:, :, :].rearrange("p k e -> p (k e)").bitcast(f32),
                                  op=ALU.subtract).then_inc(S["glo_ready"], 1)

            def route(t):
                dve.wait_ge(S["gate_done"], t + 1)
                order.done(dve.tensor_tensor(out=lg[:, :], in0=pg[:, 0:NE], in1=gb_bc[:, :], op=ALU.add))
                order.wait()
                dve.tensor_reduce(out=neg_max[:, :], in_=lg[:, :], axis=AX, op=ALU.max, negate=True
                                  ).then_inc(S["lmax_ready"], 1)
                mine = lg[:, :].unsqueeze(2).to_broadcast([P, NE, NE])
                other = lg[:, :].unsqueeze(1).to_broadcast([P, NE, NE])
                dve.tensor_tensor(out=greater[:, :, :], in0=other, in1=mine, op=ALU.is_gt)
                order.done(dve.tensor_tensor(out=equal[:, :, :], in0=other, in1=mine, op=ALU.is_equal))
                order.wait()
                order.done(dve.tensor_tensor(out=equal[:, :, :], in0=equal[:, :, :], in1=before[:, :, :], op=ALU.mult))
                order.wait()
                order.done(dve.tensor_tensor(out=greater[:, :, :], in0=greater[:, :, :], in1=equal[:, :, :], op=ALU.add))
                order.wait()
                order.done(dve.tensor_reduce(out=rank[:, :], in_=greater[:, :, :], axis=AX, op=ALU.add))
                dve.wait_ge(S["expl_ready"], t + 1)
                order.done(dve.reciprocal(exp_sum[:, 1:2], exp_sum[:, 0:1]))
                order.wait()
                order.done(dve.scalar_tensor_tensor(out=rank[:, :], in0=rank[:, :], scalar=1.5, in1=exp_l[:, :],
                                                    op0=ALU.is_lt, op1=ALU.mult))
                order.wait()
                order.done(dve.tensor_scalar(out=x_w[:, 0:NE], in0=rank[:, :], scalar1=exp_sum[:, 1:2],
                                             scalar2=0.5, op0=ALU.mult, op1=ALU.mult))
                order.wait()
                four = x_w_hl[:, :].rearrange("p (r c) -> p r c", r=2)
                w2 = x_w[:, :].unsqueeze(1).to_broadcast([P, 2, NX])
                order.done(dve.tensor_copy(four[:, :, 0:NX], w2))
                order.wait()
                order.done(dve.tensor_tensor(out=four[:, :, NX:2 * NX], in0=w2,
                                             in1=four[:, :, 0:NX].bitcast(f32), op=ALU.subtract))

            def glu(t):
                dve.wait_ge(S["up_done"], t + 1)
                dve.tensor_tensor(out=p1[:, :], in0=pu[:, 0:G], in1=b1_bc[:, :], op=ALU.add
                                  ).then_inc(S["p1_ready"], 1)
                dve.tensor_tensor(out=p2[:, :], in0=pu[:, G:2 * G], in1=b2_bc[:, :], op=ALU.add
                                  ).then_inc(S["pu_free"], 1)
                dve.wait_ge(S["th_ready"], t + 1)
                order.done(dve.scalar_tensor_tensor(out=p1[:, :], in0=th[:, :], scalar=1.0, in1=p1[:, :],
                                                    op0=ALU.add, op1=ALU.mult))
                order.wait()
                dve.wait_ge(S["pu_free"], t + 1)
                order.done(dve.tensor_tensor(out=p1[:, :], in0=p1[:, :], in1=p2[:, :], op=ALU.mult))
                order.wait()
                dve.tensor_tensor(out=p1[:, :].rearrange("p (e h) -> p e h", h=H),
                                  in0=p1[:, :].rearrange("p (e h) -> p e h", h=H),
                                  in1=x_w[:, :].unsqueeze(2).to_broadcast([P, NX, H]), op=ALU.mult
                                  ).then_inc(S["glu_ready"], 1)

            def output(t, u, turn):
                dve.wait_ge(S["d_done"], t + 1)
                dve.wait_ge(stored[u], 16 * turn)
                dve.tensor_tensor(out=out_t[:, u, :], in0=dp[:, :], in1=x1[:, u, :], op=ALU.add
                                  ).then_inc(S["out_ready"], 1)

            dve.wait_ge(S["acc_written"], 16 * (ZN + CH))
            order.done(dve.memset(x_w_hl[:, :].bitcast(f32), 0.0))
            order.done(dve.memset(x_w[:, NE:NX], 0.5 / NS))
            order.wait()
            front(0, 0, 0)
            xnT(0)
            for k in range(KG):
                dve.wait_ge(S["dnhi_ready"], k + 1)
                dve.tensor_tensor(out=dn_lo[:, k, :], in0=out_t[:, k % 3, :],
                                  in1=dn_hi[:, k, :].bitcast(f32), op=ALU.subtract).then_inc(S["dn_ready"], 1)
            dve.wait_ge(S["obhi_ready"], 1)
            dve.scalar_tensor_tensor(out=ob_hl[32:KB, :], in0=ob_raw[32:KB, :], scalar=2.0,
                                     in1=ob_hl[32:KB, :].bitcast(f32), op0=ALU.mult, op1=ALU.subtract
                                     ).then_inc(S["dn_ready"], 1)
            dve.wait_ge(S["const_ready"], 4)

            def step(t, u, turn):
                last = isinstance(t, int) and t == TL - 1
                first = isinstance(t, int) and t == 0
                if not first:
                    gT(t - 1)
                if not last:
                    front(t + 1, (u + 1) % 3, turn + (u + 1) // 3)
                route(t)
                glu(t)
                if not last:
                    xnT(t + 1)
                if not first:
                    output(t - 1, (u - 1) % 3, turn + (u - 1) // 3)

            for t in range(4):
                step(t, t % 3, t // 3)
            with dve.Fori(0, (TL - 7) // 3) as j:
                order.enter(j, 3 * NODE_STEPS)
                for v in range(4, 7):
                    step(j * 3 + v, v % 3, j + v // 3)
            order.leave((TL - 7) // 3)
            for t in range(TL - 3, TL):
                step(t, t % 3, t // 3)
            gT(TL - 1)
            output(TL - 1, (TL - 1) % 3, (TL - 1) // 3)

        @block.tensor
        def _(pe):
            def product(out_ap, hi, lo, w_hi_ap, w_lo_ap, width, first, last):
                pieces = [(c, min(c + HALF, width)) for c in range(0, width, HALF)]
                for left, right, s, e in ((hi, w_hi_ap, first, False), (hi, w_lo_ap, False, False),
                                          (lo, w_hi_ap, False, last)):
                    for c0, c1 in pieces:
                        mm = pe.matmul(out_ap[:, c0:c1], left, right[:, c0:c1], start=s, stop=e)
                return mm

            pe.wait_ge(S["const_ready"], 3)
            pe.wait_ge(S["w_split"], KD)
            for l in range(2):
                for k in range(KD):
                    last = pe.matmul(hp[l][:, k * P:(k + 1) * P], u_col[:, l, k:k + 1].to_broadcast([P, P]),
                                     ident[:, :], start=True, stop=True)
                last.then_inc(S["u_ps"], 1)

            def aggregate(k):
                pe.wait_ge(S["split_ready"], k + 1)
                for d in range(KD):
                    for part in (x_hi, x_lo):
                        pe.matmul(agg[:, d * P:(d + 1) * P], part[:, d * P:(d + 1) * P], same[:, :],
                                  start=part is x_hi, stop=part is x_lo)
                pe.matmul(e_sum[:, 0:1], same[:, :].bitcast(f32), e_w[:, :], start=True, stop=True
                          ).then_inc(S["agg_done"], 1)

            def times_w(k, s):
                pe.wait_ge(S["agglo_ready"], k + 1)
                pe.wait_ge(S["hp_free"], k + 1)
                for d in range(KD):
                    mm = product(hp[s], aggT_hi[:, s, d, :], aggT_lo[:, s, d, :], w_hi[:, d, :],
                                 w_lo[:, d, :], D, d == 0, d == KD - 1)
                mm.then_inc(S["wmm_done"], 1)

            aggregate(0)
            with pe.Fori(0, CH // 2) as j:
                for s in range(2):
                    aggregate(j * 2 + (s + 1))
                    times_w(j * 2 + s, s)
            times_w(CH - 1, 0)

            def transpose_xn(t):
                pe.wait_ge(S["xn_ready"], t + 1)
                if not isinstance(t, int) or t >= 2:
                    pe.wait_ge(S["glo_ready"], t - 1)
                for d in range(KD):
                    last = pe.transpose(tp[:, d * P:(d + 1) * P], xn[:, d * P:(d + 1) * P], ident[:, :])
                last.then_inc(S["t_done"], 1)

            def expert_up(t):
                pe.wait_ge(S["xlo_n"], t + 1)
                pe.wait_ge(S["pu_free"], t)
                for d in range(KD):
                    mm = product(pg, xnT_hi[:, d, :], xnT_lo[:, d, :], up_hi[:, d, 2 * G:UP],
                                 up_lo[:, d, 2 * G:UP], NE, d == 0, d == KD - 1)
                mm.then_inc(S["gate_done"], 1)
                for d in range(KD):
                    mm = product(pu, xnT_hi[:, d, :], xnT_lo[:, d, :], up_hi[:, d, :],
                                 up_lo[:, d, :], 2 * G, d == 0, d == KD - 1)
                mm.then_inc(S["up_done"], 1)

            def transpose_glu(t):
                pe.wait_ge(S["glu_ready"], t + 1)
                if isinstance(t, int) and t == TL - 1:
                    pass
                else:
                    pe.wait_ge(S["xlo_n"], t + 2)
                for g in range(KG):
                    pe.transpose(tp[:, g * P:(g + 1) * P], p1[:, g * P:(g + 1) * P], ident[:, :])
                pe.transpose(tp[0:KB, G:G + P], x_w_hl[:, :].bitcast(f32), ident[:, :]
                             ).then_inc(S["v_done"], 1)

            def expert_down(t):
                pe.wait_ge(S["glo_ready"], t + 1)
                pe.wait_ge(S["out_ready"], t)
                for g in range(KG):
                    product(dp, gT_hi[:, g, :], gT_lo[:, g, :], dn_hi[:, g, :], dn_lo[:, g, :],
                            D, g == 0, False)
                for c in range(2):
                    mm = pe.matmul(dp[:, c * HALF:(c + 1) * HALF], wT[:, :],
                                   ob_hl[:, c * HALF:(c + 1) * HALF], start=False, stop=True)
                mm.then_inc(S["d_done"], 1)

            transpose_xn(0)
            expert_up(0)
            transpose_xn(1)
            transpose_glu(0)
            pe.wait_ge(S["dn_ready"], KG + 1)

            def step(t):
                expert_up(t)
                if not isinstance(t, int) or t < TL - 1:
                    transpose_xn(t + 1)
                expert_down(t - 1)
                transpose_glu(t)

            step(1)
            with pe.Fori(2, TL - 1) as t:
                step(t)
            step(TL - 1)
            expert_down(TL - 1)





def kernel(x, src, dst, L0_gnn_W, L0_gnn_a, L0_ffn_gate_w, L0_ffn_gate_b, L0_ffn_rw1, L0_ffn_rb1,
           L0_ffn_rw2, L0_ffn_rb2, L0_ffn_rw3, L0_ffn_rb3, L0_ffn_sw1, L0_ffn_sb1, L0_ffn_sw2,
           L0_ffn_sb2, L0_ffn_sw3, L0_ffn_sb3):
    import numpy as np
    import concourse.bacc as bacc
    from concourse.bass_utils import run_bass_kernel_spmd

    def columns(w1):
        return np.asarray(w1).transpose(1, 0, 2).reshape(D, -1)

    idx = np.zeros((CH * P, 3), np.int32)
    idx[:, 0] = PAD_KEY
    idx[:E, 0] = np.asarray(src)
    idx[:E, 1] = np.asarray(src)
    idx[:E, 2] = np.asarray(dst)
    up = np.concatenate([columns(L0_ffn_rw1), columns(L0_ffn_sw1), columns(L0_ffn_rw2),
                         columns(L0_ffn_sw2), np.asarray(L0_ffn_gate_w)], axis=1)
    ins = {
        "x": np.asarray(x), "idx": idx, "keys": idx[:, 0], "w": np.asarray(L0_gnn_W), "a": np.asarray(L0_gnn_a),
        "up": up.reshape(KD, P, UP).transpose(1, 0, 2), "gate_b": np.asarray(L0_ffn_gate_b),
        "b1": np.concatenate([np.asarray(L0_ffn_rb1).ravel(), np.asarray(L0_ffn_sb1).ravel()]),
        "b2": np.concatenate([np.asarray(L0_ffn_rb2).ravel(), np.asarray(L0_ffn_sb2).ravel()]),
        "dn": np.concatenate([np.asarray(L0_ffn_rw3).reshape(-1, D), np.asarray(L0_ffn_sw3).reshape(-1, D)]),
        "ob": np.concatenate([np.asarray(L0_ffn_rb3), np.asarray(L0_ffn_sb3)]),
    }
    nc = bacc.Bacc("TRN2", target_bir_lowering=False, num_devices=1)
    arrays, aps = {}, []
    for name, value in ins.items():
        value = np.ascontiguousarray(value)
        arrays[f"in_{name}"] = value
        aps.append(nc.dram_tensor(f"in_{name}", value.shape, mybir.dt.from_np(value.dtype),
                                  kind="ExternalInput").ap())
    aps.append(nc.dram_tensor("out_0", (N, D), mybir.dt.float32, kind="ExternalOutput").ap())
    build(nc, *aps)
    return run_bass_kernel_spmd(nc, [arrays], core_ids=[0]).results[0]["out_0"]
```

```python
import concourse.bass as bass
from concourse import mybir
from contextlib import ExitStack

N = 10000
E = 10000
D = 1024
NE, NS, H = 8, 2, 64
NX = NE + NS
G = NX * H
P = 128
KD = D // P
KG = G // P
UP = 2 * G + NE
CH = -(-E // P)
TL = -(-N // P)
ROW = D + 16
SKIP = 16384
UPN = (CH - 3) // 2
UPW = 2 * -(-KD * UP // (2 * UPN))
SLOPE = 0.1
EPS_ROW = 1e-5
EPS_LN = 1e-5
KB = 64
HALF = D // 2
EDGE_STEPS = 10
NODE_STEPS = 19


class Order:

    def __init__(self, eng, sem):
        self.eng, self.sem, self.base, self.n = eng, sem, 0, 0

    def done(self, instruction):
        instruction.then_inc(self.sem, 1)
        self.n += 1
        return instruction

    def wait(self):
        self.eng.wait_ge(self.sem, self.base + self.n)

    def enter(self, j, steps):
        self.before, self.steps = self.base + self.n, steps
        self.base, self.n = self.before + j * steps, 0

    def leave(self, turns):
        assert self.n == self.steps, (self.n, self.steps)
        self.base, self.n = self.before + turns * self.steps, 0


def build(nc, x, idx, keys, where0, w, a, up, gate_b, b1, b2, dn, ob, out):
    f32, f32r, i32, bf16 = mybir.dt.float32, mybir.dt.float32r, mybir.dt.int32, mybir.dt.bfloat16
    ALU = mybir.AluOpType
    ACT = mybir.ActivationFunctionType
    AX = mybir.AxisListType.X

    acc = nc.dram_tensor("acc", [CH * P, ROW], f32).ap()
    where = nc.dram_tensor("where", [N + 16, 1], i32).ap()
    w_rows = w.rearrange("(k p) n -> p k n", p=P)
    dn_rows = dn.rearrange("(k p) n -> p k n", p=P)

    whole, edges, nodes = ExitStack(), ExitStack(), ExitStack()
    with whole:
        def sem(name):
            return whole.enter_context(nc.semaphore(name))

        def tile(stack, name, shape, dt=f32):
            return stack.enter_context(nc.sbuf_tensor(name, shape, dt))

        def bank(stack, name, shape):
            return stack.enter_context(nc.psum_tensor(name, shape, f32))

        ident = tile(whole, "ident", [P, P])
        below = tile(whole, "below", [P, P])
        up_hi = tile(whole, "up_hi", [P, UPN * UPW], f32r)
        up_lo = tile(whole, "up_lo", [P, UPN * UPW], f32r)
        minus_half = tile(whole, "minus_half", [P, 2])
        stats = tile(whole, "stats", [P, 2, 12])
        mean_var = tile(whole, "mean_var", [P, 2, 2])
        var_eps = tile(whole, "var_eps", [P, 2])
        rstd = tile(whole, "rstd", [P, 2])
        affine = tile(whole, "affine", [P, 2])

        with edges:
            w_hi = tile(edges, "w_hi", [P, KD, D], f32r)
            w_lo = tile(edges, "w_lo", [P, KD, D], f32r)
            u_bc = tile(edges, "u_bc", [P, 2, D])
            u_sum = tile(edges, "u_sum", [P, 2])
            junk = tile(edges, "junk", [P, D], bf16)
            up_raw = tile(edges, "up_raw", [P, UPW])
            result = tile(edges, "result", [P, 2, ROW])
            with ExitStack() as staging:
                w_raw = tile(staging, "w_raw", [P, KD, D])
                a_bc = tile(staging, "a_bc", [P, 2, D])
                u_col = tile(staging, "u_col", [P, 2, KD])
            src_rows = tile(edges, "src_rows", [P, 2, D])
            dst_rows = tile(edges, "dst_rows", [P, 2, D])
            x_hi = tile(edges, "x_hi", [P, D], f32r)
            x_lo = tile(edges, "x_lo", [P, D], f32r)
            same = tile(edges, "same", [P, 2, P], f32r)
            aggT_hi = tile(edges, "aggT_hi", [P, 2, KD, P], f32r)
            aggT_lo = tile(edges, "aggT_lo", [P, 2, KD, P], f32r)
            edge_idx = [tile(edges, f"edge_idx{s}", [P, 4], i32) for s in range(2)]
            src_keys = tile(edges, "src_keys", [P, 2, P], i32)
            add_idx = [tile(edges, f"add_idx{s}", [P, 1], i32) for s in range(2)]
            first_idx = [tile(edges, f"first_idx{s}", [P, 1], i32) for s in range(2)]
            edge_no = [tile(edges, f"edge_no{s}", [P, 1], i32) for s in range(2)]
            where_e = [tile(edges, f"where_e{s}", [P, 1], i32) for s in range(2)]
            src_key = tile(edges, "src_key", [P, 1])
            earlier = tile(edges, "earlier", [P, 1])
            dots = tile(edges, "dots", [P, 2])
            mean_u = tile(edges, "mean_u", [P, 2])
            logit = tile(edges, "logit", [P, 1])
            e_w = tile(edges, "e_w", [P, 2, 1])
            skip = tile(edges, "skip", [P, 1])
            first_row = tile(edges, "first_row", [P, 1])
            add_row = tile(edges, "add_row", [P, 2, 1])
            sum_row = tile(edges, "sum_row", [P, 2, 2])
            with ExitStack() as banks:
                agg = bank(banks, "agg", [P, D])
                hp = [bank(banks, f"hp{s}", [P, D]) for s in range(2)]
                e_sum = bank(banks, "e_sum", [P, HALF])

        with nodes:
            dn_hi = tile(nodes, "dn_hi", [P, KG, D], f32r)
            dn_lo = tile(nodes, "dn_lo", [P, KG, D], f32r)
            ob_raw = tile(nodes, "ob_raw", [KB, D])
            ob_hl = tile(nodes, "ob_hl", [KB, D], f32r)
            acc_t = tile(nodes, "acc_t", [P, 3, ROW])
            x1 = tile(nodes, "x1", [P, 3, D])
            out_t = tile(nodes, "out_t", [P, 3, D])
            exp_y = tile(nodes, "exp_y", [P, D])
            xn = tile(nodes, "xn", [P, D])
            xnT_hi = tile(nodes, "xnT_hi", [P, KD, P], f32r)
            xnT_lo = tile(nodes, "xnT_lo", [P, KD, P], f32r)
            p1 = tile(nodes, "p1", [P, G])
            p2 = tile(nodes, "p2", [P, G])
            th = tile(nodes, "th", [P, G])
            gT_hi = tile(nodes, "gT_hi", [P, KG, P], f32r)
            gT_lo = tile(nodes, "gT_lo", [P, KG, P], f32r)
            wT = tile(nodes, "wT", [KB, P], f32r)
            b1_bc = tile(nodes, "b1_bc", [P, G])
            b2_bc = tile(nodes, "b2_bc", [P, G])
            gb_bc = tile(nodes, "gb_bc", [P, NE])
            den = tile(nodes, "den", [P, 3])
            where_t = [tile(nodes, f"where_t{u}", [P, 1], i32) for u in range(3)]
            lg = tile(nodes, "lg", [P, NE])
            greater = tile(nodes, "greater", [P, NE, NE])
            equal = tile(nodes, "equal", [P, NE, NE])
            before = tile(nodes, "before", [P, NE, NE])
            rank = tile(nodes, "rank", [P, NE])
            neg_max = tile(nodes, "neg_max", [P, 1])
            exp_l = tile(nodes, "exp_l", [P, NE])
            exp_sum = tile(nodes, "exp_sum", [P, 2])
            x_w = tile(nodes, "x_w", [P, NX])
            x_w_hl = tile(nodes, "x_w_hl", [P, KB], f32r)
            with ExitStack() as banks:
                tp = bank(banks, "tp", [P, D])
                pu = bank(banks, "pu", [P, 3 * HALF])
                dp = bank(banks, "dp", [P, D])

        names = """const_ready a_loaded w_split u_cols u_ps u_bc_ready setup_done
            split_ready agglo_ready agghi_ready agg_done wmm_done hp_free result_ready res_free
            acc_added where_begun where_read where_written first_ready idx_used up_loaded up_split uphi_ready
            var_ready rstd_ready logit_ready e_ready scale_ready xhi_ready
            dnhi_ready dn_ready consts_loaded ob_zero acct_zero rinv_ready expy_ready norm_ready xn_ready
            t_done xhi_n xlo_n gate_done up_done pu_free p1_ready th_ready glu_ready v_done
            ghi_ready glo_ready d_done out_ready lmax_ready expl_ready
            stats_done gathers_begun whi_ready obhi_ready
            vector_step scalar_step pool_step""".split()
        S = {n: sem(n) for n in names}
        w_loaded = [sem(f"w_loaded{i}") for i in range(KD)]
        dn_loaded = [sem(f"dn_loaded{i}") for i in range(3)]
        idx_loaded = [sem(f"idx_loaded{i}") for i in range(2)]
        gathered = [sem(f"gathered{i}") for i in range(2)]
        rows_stored = [sem(f"rows_stored{i}") for i in range(2)]
        x_loaded = [sem(f"x_loaded{i}") for i in range(3)]
        where_loaded = [sem(f"where_loaded{i}") for i in range(3)]
        acc_loaded = [sem(f"acc_loaded{i}") for i in range(3)]
        stored = [sem(f"stored{i}") for i in range(3)]
        block = whole.enter_context(nc.Block())

        def row0(t):
            return N - P if isinstance(t, int) and t == TL - 1 else t * P

        @block.sync
        def _(sp):
            for k in range(KD):
                sp.dma_start(w_raw[:, k, :], w_rows[:, k, :]).then_inc(w_loaded[k], 16)
                if k == 0:
                    sp.dma_start(a_bc[:, :, :], a.rearrange("o (l n) -> (o l) n", l=2).partition_broadcast(P)
                                 ).then_inc(S["a_loaded"], 16)
            sp.dma_start(where.rearrange("(a b) o -> a (b o)", a=16), where0.rearrange("(a b) -> a b", a=16)
                         ).then_inc(S["where_begun"], 16)

            def load_indices(k, s):
                sp.dma_start(edge_idx[s][:, :], idx[bass.ds(k * P, P), :]).then_inc(idx_loaded[s], 16)
                sp.dma_start(src_keys[:, s, :],
                             keys[bass.ds(k * P, P)].partition_broadcast(P)
                             ).then_inc(idx_loaded[s], 16)

            def store_rows(k, s):
                sp.wait_ge(S["result_ready"], k + 1)
                sp.dma_start(acc[bass.ds(k * P, P), :], result[:, s, :]).then_inc(rows_stored[s], 16)

            load_indices(0, 0)
            load_indices(1, 1)
            sp.wait_ge(S["idx_used"], 1)
            load_indices(2, 0)
            sp.wait_ge(S["idx_used"], 2)
            load_indices(3, 1)
            with sp.Fori(0, UPN - 1) as j:
                sp.wait_ge(S["up_split"], j + 1)
                sp.dma_start(up_raw[:, :], up[:, bass.ds(j * UPW, UPW)]).then_inc(S["up_loaded"], 16)
                for s in range(2):
                    sp.wait_ge(S["idx_used"], j * 2 + (s + 3))
                    load_indices(j * 2 + (s + 4), s)
                    store_rows(j * 2 + s, s)
            sp.wait_ge(S["up_split"], UPN)
            sp.dma_start(up_raw[:, :], up[:, (UPN - 1) * UPW:]).then_inc(S["up_loaded"], 16)
            sp.wait_ge(S["idx_used"], CH - 2)
            load_indices(CH - 1, (CH - 1) % 2)
            for k in range(CH - 5, CH):
                store_rows(k, k % 2)

            def load_x(t, u):
                sp.dma_start(x1[:, u, :], x[bass.ds(row0(t), P), :]).then_inc(x_loaded[u], 16)

            def load_where(t, u):
                sp.dma_start(where_t[u][:, :], where[bass.ds(row0(t), P), :]).then_inc(where_loaded[u], 16)

            def store_tile(t, u):
                if isinstance(t, int) and t == TL - 1:
                    new = N - (TL - 1) * P
                    sp.dma_start(out[N - new:N, :], out_t[P - new:P, u, :]).then_inc(stored[u], 16)
                else:
                    sp.dma_start(out[bass.ds(row0(t), P), :], out_t[:, u, :]).then_inc(stored[u], 16)

            sp.wait_ge(S["where_written"], 16 * CH)
            sp.wait_ge(S["acc_added"], 16 * CH)
            sp.wait_ge(rows_stored[0], 16 * (CH - CH // 2))
            sp.wait_ge(rows_stored[1], 16 * (CH // 2))
            for t in range(3):
                load_where(t, t)
                load_x(t, t)
            for k in range(KG):
                if k >= 3:
                    sp.wait_ge(S["dn_ready"], k - 2)
                sp.dma_start(out_t[:, k % 3, :], dn_rows[:, k, :]).then_inc(dn_loaded[k % 3], 16)
            sp.wait_ge(S["ob_zero"], 1)
            for r in (0, NX, 32, 32 + NX):
                sp.dma_start(ob_raw[r:r + NX, :], ob).then_inc(S["consts_loaded"], 16)
            sp.dma_start(b1_bc[:, :], b1.partition_broadcast(P)).then_inc(S["consts_loaded"], 16)
            sp.dma_start(b2_bc[:, :], b2.partition_broadcast(P)).then_inc(S["consts_loaded"], 16)
            sp.dma_start(gb_bc[:, :], gate_b.partition_broadcast(P)).then_inc(S["consts_loaded"], 16)
            sp.wait_ge(S["norm_ready"], 1)
            load_where(3, 0)
            with sp.Fori(0, (TL - 7) // 3) as j:
                for u in range(3):
                    sp.wait_ge(S["out_ready"], j * 3 + u + 1)
                    load_x(j * 3 + (u + 3), u)
                    load_where(j * 3 + (u + 4), (u + 1) % 3)
                    store_tile(j * 3 + u, u)
            for t in range(TL - 7, TL):
                sp.wait_ge(S["out_ready"], t + 1)
                if t + 3 < TL:
                    load_x(t + 3, t % 3)
                if t + 4 < TL:
                    load_where(t + 4, (t + 1) % 3)
                store_tile(t, t % 3)
            for u in range(3):
                sp.wait_ge(stored[u], 16 * len(range(u, TL, 3)))

        @block.gpsimd
        def _(pool):
            order = Order(pool, S["pool_step"])
            order.done(pool.memset(ident[:, :], 0.0))
            order.done(pool.memset(below[:, :], 1.0))
            pool.memset(minus_half[:, :], -0.5).then_inc(S["const_ready"], 1)
            order.wait()
            pool.affine_select(out=ident[:, :], in_=ident[:, :], compare_op=ALU.not_equal, fill=1.0,
                               base=0, pattern=[[-1, P]], channel_multiplier=1).then_inc(S["const_ready"], 1)
            pool.affine_select(out=below[:, :], in_=below[:, :], compare_op=ALU.is_gt, fill=0.0,
                               base=0, pattern=[[-1, P]], channel_multiplier=1).then_inc(S["const_ready"], 1)
            def gather(k, s, turn):
                pool.wait_ge(idx_loaded[s], 32 * (turn + 1))
                pool.sem_inc(S["gathers_begun"], 1)
                for rows, col in ((src_rows, 1), (dst_rows, 2)):
                    pool.indirect_dma_start(
                        out=rows[:, s, :], out_offset=None, in_=x,
                        in_offset=bass.IndirectOffsetOnAxis(ap=edge_idx[s][:, col:col + 1], axis=0)
                        ).then_inc(gathered[s], 16)

            def power(k):
                pool.wait_ge(S["var_ready"], k + 1)
                pool.tensor_tensor(out=rstd[:, :], in0=var_eps[:, :], in1=minus_half[:, :],
                                   op=ALU.pow).then_inc(S["rstd_ready"], 1)

            def read_where(k, s, turn):
                pool.wait_ge(idx_loaded[s], 32 * (turn + 1))
                if isinstance(k, int) and k == 0:
                    pool.wait_ge(S["where_begun"], 16)
                else:
                    pool.wait_ge(S["where_written"], k * 16)
                pool.sem_inc(S["gathers_begun"], 1)
                pool.indirect_dma_start(
                    out=where_e[s][:, :], out_offset=None, in_=where,
                    in_offset=bass.IndirectOffsetOnAxis(ap=edge_idx[s][:, 0:1], axis=0)
                    ).then_inc(S["where_read"], 16)

            def write_where(k, s):
                pool.wait_ge(S["first_ready"], k + 1)
                pool.wait_ge(S["where_read"], (k + 1) * 16)
                pool.sem_inc(S["idx_used"], 1)
                pool.indirect_dma_start(
                    out=where, out_offset=bass.IndirectOffsetOnAxis(ap=first_idx[s][:, :], axis=0),
                    in_=edge_no[s][:, :], in_offset=None, bounds_check=N - 1, oob_is_err=False
                    ).then_inc(S["where_written"], 16)

            def add_rows(k, s, turn):
                pool.wait_ge(S["result_ready"], k + 1)
                if not isinstance(k, int) or k > 0:
                    pool.wait_ge(rows_stored[1 - s], (turn + 1) * 16)
                    pool.wait_ge(S["acc_added"], k * 16)
                pool.sem_inc(S["res_free"], 1)
                pool.indirect_dma_start(
                    out=acc, out_offset=bass.IndirectOffsetOnAxis(ap=add_idx[s][:, :], axis=0),
                    in_=result[:, s, :], in_offset=None, bounds_check=CH * P - 1, oob_is_err=False,
                    compute_op=ALU.add).then_inc(S["acc_added"], 16)

            pool.sem_inc(S["res_free"], 1)
            pool.wait_ge(S["setup_done"], 1)
            gather(0, 0, 0)
            gather(1, 1, 0)
            read_where(0, 0, 0)
            power(0)
            write_where(0, 0)

            def edge_step(p, s, turn):
                pool.wait_ge(S["split_ready"], p + 1)
                read_where(p + 1, 1 - s, turn + s)
                power(p + 1)
                if not isinstance(p, int) or p + 2 < CH:
                    gather(p + 2, s, turn + 1)
                if not isinstance(p, int) or p >= 2:
                    add_rows(p - 2, s, turn - 1 - (1 - s))
                write_where(p + 1, 1 - s)

            for p in range(4):
                edge_step(p, p % 2, p // 2)
            with pool.Fori(0, (CH - 7) // 2) as j:
                for s in range(2):
                    edge_step(j * 2 + (s + 4), s, j + 2)
            for p in range(CH - 3, CH - 1):
                edge_step(p, p % 2, p // 2)
            for k in range(CH - 3, CH):
                add_rows(k, k % 2, (k - 1) // 2)

            pool.wait_ge(S["acc_added"], 16 * CH)
            pool.wait_ge(rows_stored[(CH - 1) % 2], 16 * (CH - CH // 2))
            pool.memset(acc_t[:, :, :], 0.0).then_inc(S["acct_zero"], 1)
            pool.wait_ge(S["acct_zero"], 1)

            def gather_acc(t, u, turn):
                pool.wait_ge(where_loaded[u], (turn + 1) * 16)
                pool.sem_inc(S["gathers_begun"], 1)
                pool.indirect_dma_start(
                    out=acc_t[:, u, :], out_offset=None, in_=acc,
                    in_offset=bass.IndirectOffsetOnAxis(ap=where_t[u][:, :], axis=0),
                    bounds_check=CH * P - 1, oob_is_err=False).then_inc(acc_loaded[u], 16)

            for t in range(3):
                gather_acc(t, t, 0)
            pool.memset(ob_raw[:, :], 0.0).then_inc(S["ob_zero"], 1)
            order.done(pool.memset(before[:, :, :], 1.0))
            order.wait()
            pool.affine_select(out=before[:, :, :], in_=before[:, :, :], compare_op=ALU.is_gt, fill=0.0,
                               base=0, pattern=[[1, NE], [-1, NE]], channel_multiplier=0
                               ).then_inc(S["const_ready"], 1)
            power(CH)
            power(CH + 1)
            with pool.Fori(0, (TL - 4) // 3) as j:
                for u in range(3):
                    pool.wait_ge(S["norm_ready"], j * 3 + (u + 1))
                    gather_acc(j * 3 + (u + 3), u, j + 1)
                    power(j * 3 + (u + 2 + CH))
            gather_acc(TL - 1, (TL - 1) % 3, (TL - 1) // 3)
            for t in range(TL - 2, TL):
                power(CH + t)

        @block.scalar
        def _(act):
            order = Order(act, S["scalar_step"])
            act.wait_ge(S["const_ready"], 3)
            for k in range(KD):
                act.wait_ge(w_loaded[k], 16)
                act.activation(w_hi[:, k, :], w_raw[:, k, :], ACT.Copy).then_inc(S["whi_ready"], 1)
            for l in range(2):
                act.wait_ge(S["u_ps"], l + 1)
                act.activation(u_bc[:, l, :], hp[l][:, :], ACT.Copy).then_inc(S["u_bc_ready"], 1)
            act.wait_ge(S["u_bc_ready"], 2)
            act.sem_inc(S["hp_free"], 2)

            def edge_rows(k, s):
                act.wait_ge(S["logit_ready"], k + 1)
                act.activation(e_w[:, s, :], logit[:, :], ACT.Exp, scale=-1.0).then_inc(S["e_ready"], 1)
                act.wait_ge(S["scale_ready"], k + 1)
                order.done(act.activation(dst_rows[:, s, :], dst_rows[:, s, :], ACT.Identity,
                                          scale=affine[:, 0:1], bias=affine[:, 1:2]))
                order.wait()
                act.activation(x_hi[:, :], dst_rows[:, s, :], ACT.Copy).then_inc(S["xhi_ready"], 1)

            def agg_hi(k, s):
                act.wait_ge(S["agg_done"], k + 1)
                act.activation(aggT_hi[:, s, :, :].rearrange("p k e -> p (k e)"), agg[:, :], ACT.Copy
                               ).then_inc(S["agghi_ready"], 1)

            def evacuate(k, s):
                act.wait_ge(S["wmm_done"], k + 1)
                act.wait_ge(S["res_free"], k + 1)
                act.activation(result[:, s, 0:D], hp[s][:, :], ACT.Copy).then_inc(S["hp_free"], 1)
                act.activation(result[:, s, D:D + 1], sum_row[:, s, 0:1], ACT.Copy)
                act.activation(add_idx[s][:, :], sum_row[:, s, 1:2], ACT.Copy).then_inc(S["result_ready"], 1)

            def edge_step(p, s):
                if not isinstance(p, int) or p >= 2:
                    evacuate(p - 2, s)
                agg_hi(p, s)
                if not isinstance(p, int) or p + 1 < CH:
                    edge_rows(p + 1, 1 - s)

            edge_rows(0, 0)
            edge_step(0, 0)
            edge_step(1, 1)
            with act.Fori(0, UPN) as j:
                order.enter(j, 2)
                act.wait_ge(S["up_loaded"], (j + 1) * 16)
                act.wait_ge(S["up_split"], j + 1)
                act.activation(up_hi[:, bass.ds(j * UPW, UPW)], up_raw[:, :], ACT.Copy
                               ).then_inc(S["uphi_ready"], 1)
                for s in range(2):
                    edge_step(j * 2 + (s + 2), s)
            order.leave(UPN)
            edge_step(CH - 1, 0)
            evacuate(CH - 2, 1)
            evacuate(CH - 1, 0)

            def front(t, u):
                act.wait_ge(S["rinv_ready"], t + 1)
                act.activation(exp_y[:, :], acc_t[:, u, 0:D], ACT.Exp, scale=den[:, 2:3]
                               ).then_inc(S["expy_ready"], 1)
                act.wait_ge(S["norm_ready"], t + 1)
                act.activation(xn[:, :], x1[:, u, :], ACT.Identity, scale=affine[:, 0:1],
                               bias=affine[:, 1:2]).then_inc(S["xn_ready"], 1)

            def xnT(t):
                act.wait_ge(S["t_done"], t + 1)
                act.activation(xnT_hi[:, :, :].rearrange("p k e -> p (k e)"), tp[:, :], ACT.Copy
                               ).then_inc(S["xhi_n"], 1)

            def gT(t):
                act.wait_ge(S["v_done"], t + 1)
                act.activation(gT_hi[:, :, :].rearrange("p k e -> p (k e)"), tp[:, 0:G], ACT.Copy
                               ).then_inc(S["ghi_ready"], 1)

            def experts(t):
                act.wait_ge(S["lmax_ready"], t + 1)
                act.activation(exp_l[:, :], lg[:, :], ACT.Exp, bias=neg_max[:, :],
                               accum_out=exp_sum[:, 0:1]).then_inc(S["expl_ready"], 1)
                act.wait_ge(S["p1_ready"], t + 1)
                act.activation(th[:, :], p1[:, :], ACT.Tanh, scale=0.5).then_inc(S["th_ready"], 1)

            front(0, 0)
            xnT(0)
            for k in range(KG):
                act.wait_ge(dn_loaded[k % 3], 16 * (k // 3 + 1))
                act.activation(dn_hi[:, k, :], out_t[:, k % 3, :], ACT.Copy).then_inc(S["dnhi_ready"], 1)
            act.wait_ge(S["consts_loaded"], 16 * 7)
            act.activation(ob_hl[:, :], ob_raw[:, :], ACT.Copy, scale=2.0).then_inc(S["obhi_ready"], 1)

            def step(t, u):
                if not isinstance(t, int) or t > 0:
                    gT(t - 1)
                if not isinstance(t, int) or t < TL - 1:
                    front(t + 1, (u + 1) % 3)
                experts(t)
                if not isinstance(t, int) or t < TL - 1:
                    xnT(t + 1)

            step(0, 0)
            with act.Fori(0, (TL - 4) // 3) as j:
                for v in range(1, 4):
                    step(j * 3 + v, v % 3)
            for t in range(TL - 3, TL):
                step(t, t % 3)
            gT(TL - 1)

        @block.vector
        def _(dve):
            order = Order(dve, S["vector_step"])
            dve.memset(result[:, :, D:ROW], 0.0)
            dve.wait_ge(S["a_loaded"], 16)
            for k in range(KD):
                dve.wait_ge(w_loaded[k], 16)
                for l in range(2):
                    order.wait()
                    order.done(dve.tensor_tensor_reduce(
                        out=junk[:, :], in0=w_raw[:, k, :], in1=a_bc[:, l, :], scale=1.0, scalar=0.0,
                        op0=ALU.mult, op1=ALU.add, accum_out=u_col[:, l, k:k + 1]))
            dve.sem_inc(S["up_split"], 1)
            order.wait()
            dve.sem_inc(S["u_cols"], 1)
            for k in range(KD):
                dve.wait_ge(S["whi_ready"], k + 1)
                dve.tensor_tensor(out=w_lo[:, k, :], in0=w_raw[:, k, :],
                                  in1=w_hi[:, k, :].bitcast(f32), op=ALU.subtract).then_inc(S["w_split"], 1)
            dve.wait_ge(S["u_bc_ready"], 2)
            dve.tensor_reduce(out=u_sum[:, :], in_=u_bc[:, :, :], axis=AX, op=ALU.add
                              ).then_inc(S["setup_done"], 1)
            dve.wait_ge(S["setup_done"], 1)

            def logits(k, s, turn):
                def dot(r):
                    order.done(dve.tensor_tensor_reduce(
                        out=junk[:, :], in0=(src_rows, dst_rows)[r][:, s, :], in1=u_bc[:, r, :],
                        scale=1.0, scalar=0.0, op0=ALU.mult, op1=ALU.add, accum_out=dots[:, r:r + 1]))

                dve.wait_ge(gathered[s], 32 * (turn + 1))
                for r, rows in enumerate((src_rows, dst_rows)):
                    for h in range(2):
                        last = dve.bn_stats(out=stats[:, r, 6 * h:6 * h + 6],
                                            in_=rows[:, s, h * HALF:(h + 1) * HALF])
                order.done(last)
                order.wait()
                dot(0)
                for r in range(2):
                    last = dve.bn_aggr(out=mean_var[:, r, :], in_=stats[:, r, :])
                order.done(last)
                order.wait()
                dve.tensor_scalar(out=var_eps[:, :], in0=mean_var[:, :, 1], scalar1=EPS_LN, scalar2=None,
                                  op0=ALU.add).then_inc(S["var_ready"], 1)
                dot(1)
                dve.tensor_tensor(out=mean_u[:, :], in0=mean_var[:, :, 0], in1=u_sum[:, :], op=ALU.mult)
                dve.wait_ge(idx_loaded[s], 32 * (turn + 1))
                dve.tensor_copy(edge_no[s][:, :], edge_idx[s][:, 3:4])
                order.done(dve.tensor_copy(src_key[:, :], edge_idx[s][:, 0:1]))
                order.wait()
                dve.tensor_tensor(out=dots[:, :], in0=dots[:, :], in1=mean_u[:, :], op=ALU.subtract)
                order.done(dve.tensor_scalar(out=same[:, s, :], in0=src_keys[:, s, :], scalar1=src_key[:, :],
                                             scalar2=None, op0=ALU.is_equal))
                order.wait()
                order.done(dve.tensor_tensor_reduce(out=junk[:, 0:P], in0=same[:, s, :].bitcast(f32),
                                                    in1=below[:, :], scale=1.0, scalar=0.0, op0=ALU.mult,
                                                    op1=ALU.add, accum_out=earlier[:, :]))
                dve.wait_ge(S["rstd_ready"], k + 1)
                order.done(dve.tensor_tensor_reduce(out=junk[:, P:P + 2], in0=dots[:, :], in1=rstd[:, :],
                                                    scale=1.0, scalar=0.0, op0=ALU.mult, op1=ALU.add,
                                                    accum_out=logit[:, :]))
                order.wait()
                dve.scalar_tensor_tensor(out=logit[:, :], in0=logit[:, :], scalar=SLOPE, in1=logit[:, :],
                                         op0=ALU.mult, op1=ALU.max).then_inc(S["logit_ready"], 1)
                dve.wait_ge(S["where_read"], (k + 1) * 16)
                dve.tensor_scalar(out=skip[:, :], in0=where_e[s][:, :], scalar1=float(SKIP),
                                  scalar2=float(SKIP), op0=ALU.is_lt, op1=ALU.mult)
                order.done(dve.scalar_tensor_tensor(out=first_row[:, :], in0=earlier[:, :], scalar=float(SKIP),
                                                    in1=src_key[:, :], op0=ALU.mult, op1=ALU.add))
                dve.scalar_tensor_tensor(out=add_row[:, s, :], in0=earlier[:, :], scalar=float(SKIP),
                                         in1=where_e[s][:, :], op0=ALU.mult, op1=ALU.add)
                order.wait()
                dve.tensor_tensor(out=first_idx[s][:, :], in0=first_row[:, :], in1=skip[:, :], op=ALU.add
                                  ).then_inc(S["first_ready"], 1)
                dve.wait_ge(S["e_ready"], k + 1)
                order.done(dve.tensor_tensor(out=affine[:, 0:1], in0=e_w[:, s, :], in1=rstd[:, 1:2], op=ALU.mult))
                order.wait()
                dve.scalar_tensor_tensor(out=affine[:, 1:2], in0=mean_var[:, 1, 0:1], scalar=-1.0,
                                         in1=affine[:, 0:1], op0=ALU.mult, op1=ALU.mult
                                         ).then_inc(S["scale_ready"], 1)

            def x_split(k, s):
                dve.wait_ge(S["xhi_ready"], k + 1)
                dve.tensor_tensor(out=x_lo[:, :], in0=dst_rows[:, s, :], in1=x_hi[:, :].bitcast(f32),
                                  op=ALU.subtract).then_inc(S["split_ready"], 1)

            def agg_lo(k, s):
                dve.wait_ge(S["agghi_ready"], k + 1)
                dve.tensor_copy(sum_row[:, s, 0:1], e_sum[:, 0:1])
                dve.tensor_copy(sum_row[:, s, 1:2], add_row[:, s, :])
                dve.tensor_tensor(out=aggT_lo[:, s, :, :].rearrange("p k e -> p (k e)"), in0=agg[:, :],
                                  in1=aggT_hi[:, s, :, :].rearrange("p k e -> p (k e)").bitcast(f32),
                                  op=ALU.subtract).then_inc(S["agglo_ready"], 1)

            def edge_step(p, s, turn):
                if not isinstance(p, int) or p + 1 < CH:
                    logits(p + 1, 1 - s, turn + s)
                agg_lo(p, s)
                if not isinstance(p, int) or p + 1 < CH:
                    x_split(p + 1, 1 - s)

            logits(0, 0, 0)
            x_split(0, 0)
            edge_step(0, 0, 0)
            edge_step(1, 1, 0)
            with dve.Fori(0, UPN) as j:
                order.enter(j, 2 * EDGE_STEPS)
                dve.wait_ge(S["uphi_ready"], j + 1)
                dve.tensor_tensor(out=up_lo[:, bass.ds(j * UPW, UPW)], in0=up_raw[:, :],
                                  in1=up_hi[:, bass.ds(j * UPW, UPW)].bitcast(f32), op=ALU.subtract
                                  ).then_inc(S["up_split"], 1)
                for s in range(2):
                    edge_step(j * 2 + (s + 2), s, j + 1)
            order.leave(UPN)
            edge_step(CH - 1, 0, 0)

            def front(t, u, turn):
                dve.wait_ge(acc_loaded[u], 16 * (turn + 1))
                order.done(dve.tensor_scalar(out=den[:, 0:1], in0=acc_t[:, u, D:D + 1], scalar1=EPS_ROW,
                                             scalar2=None, op0=ALU.add))
                order.wait()
                order.done(dve.reciprocal(den[:, 1:2], den[:, 0:1]))
                order.wait()
                dve.scalar_tensor_tensor(out=den[:, 2:3], in0=where_t[u][:, :], scalar=float(SKIP),
                                         in1=den[:, 1:2], op0=ALU.is_lt, op1=ALU.mult
                                         ).then_inc(S["rinv_ready"], 1)
                dve.wait_ge(S["expy_ready"], t + 1)
                order.done(dve.tensor_scalar(out=exp_y[:, :], in0=exp_y[:, :], scalar1=1.0, scalar2=-1.0,
                                             op0=ALU.min, op1=ALU.add))
                order.wait()
                order.done(dve.scalar_tensor_tensor(out=acc_t[:, u, 0:D], in0=acc_t[:, u, 0:D],
                                                    scalar=den[:, 2:3], in1=exp_y[:, :],
                                                    op0=ALU.mult, op1=ALU.max))
                order.wait()
                dve.wait_ge(x_loaded[u], 16 * (turn + 1))
                order.done(dve.tensor_tensor(out=x1[:, u, :], in0=x1[:, u, :], in1=acc_t[:, u, 0:D], op=ALU.add))
                order.wait()
                for h in range(2):
                    last = dve.bn_stats(out=stats[:, 0, 6 * h:6 * h + 6],
                                        in_=x1[:, u, h * HALF:(h + 1) * HALF])
                order.done(last)
                order.wait()
                dve.sem_inc(S["stats_done"], 1)
                order.done(dve.bn_aggr(out=mean_var[:, 0, :], in_=stats[:, 0, :]))
                order.wait()
                dve.tensor_scalar(out=var_eps[:, :], in0=mean_var[:, :, 1], scalar1=EPS_LN, scalar2=None,
                                  op0=ALU.add).then_inc(S["var_ready"], 1)
                dve.wait_ge(S["rstd_ready"], t + (CH + 1))
                dve.tensor_copy(affine[:, 0:1], rstd[:, 0:1])
                dve.scalar_tensor_tensor(out=affine[:, 1:2], in0=mean_var[:, 0, 0:1], scalar=-1.0,
                                         in1=rstd[:, 0:1], op0=ALU.mult, op1=ALU.mult
                                         ).then_inc(S["norm_ready"], 1)

            def xnT(t):
                dve.wait_ge(S["xhi_n"], t + 1)
                dve.tensor_tensor(out=xnT_lo[:, :, :].rearrange("p k e -> p (k e)"), in0=tp[:, :],
                                  in1=xnT_hi[:, :, :].rearrange("p k e -> p (k e)").bitcast(f32),
                                  op=ALU.subtract).then_inc(S["xlo_n"], 1)

            def gT(t):
                dve.wait_ge(S["ghi_ready"], t + 1)
                dve.tensor_copy(wT[:, :], tp[0:KB, G:G + P])
                dve.tensor_tensor(out=gT_lo[:, :, :].rearrange("p k e -> p (k e)"), in0=tp[:, 0:G],
                                  in1=gT_hi[:, :, :].rearrange("p k e -> p (k e)").bitcast(f32),
                                  op=ALU.subtract).then_inc(S["glo_ready"], 1)

            def route(t):
                dve.wait_ge(S["gate_done"], t + 1)
                order.done(dve.tensor_tensor(out=lg[:, :], in0=pu[:, 2 * G:UP], in1=gb_bc[:, :], op=ALU.add))
                order.wait()
                dve.tensor_reduce(out=neg_max[:, :], in_=lg[:, :], axis=AX, op=ALU.max, negate=True
                                  ).then_inc(S["lmax_ready"], 1)
                mine = lg[:, :].unsqueeze(2).to_broadcast([P, NE, NE])
                other = lg[:, :].unsqueeze(1).to_broadcast([P, NE, NE])
                dve.tensor_tensor(out=greater[:, :, :], in0=other, in1=mine, op=ALU.is_gt)
                order.done(dve.tensor_tensor(out=equal[:, :, :], in0=other, in1=mine, op=ALU.is_equal))
                order.wait()
                order.done(dve.tensor_tensor(out=equal[:, :, :], in0=equal[:, :, :], in1=before[:, :, :], op=ALU.mult))
                order.wait()
                order.done(dve.tensor_tensor(out=greater[:, :, :], in0=greater[:, :, :], in1=equal[:, :, :], op=ALU.add))
                order.wait()
                order.done(dve.tensor_reduce(out=rank[:, :], in_=greater[:, :, :], axis=AX, op=ALU.add))
                dve.wait_ge(S["expl_ready"], t + 1)
                order.done(dve.reciprocal(exp_sum[:, 1:2], exp_sum[:, 0:1]))
                order.wait()
                order.done(dve.scalar_tensor_tensor(out=rank[:, :], in0=rank[:, :], scalar=1.5, in1=exp_l[:, :],
                                                    op0=ALU.is_lt, op1=ALU.mult))
                order.wait()
                order.done(dve.tensor_scalar(out=x_w[:, 0:NE], in0=rank[:, :], scalar1=exp_sum[:, 1:2],
                                             scalar2=0.5, op0=ALU.mult, op1=ALU.mult))
                order.wait()
                four = x_w_hl[:, :].rearrange("p (r c) -> p r c", r=2)
                w2 = x_w[:, :].unsqueeze(1).to_broadcast([P, 2, NX])
                order.done(dve.tensor_copy(four[:, :, 0:NX], w2))
                order.wait()
                order.done(dve.tensor_tensor(out=four[:, :, NX:2 * NX], in0=w2,
                                             in1=four[:, :, 0:NX].bitcast(f32), op=ALU.subtract))

            def glu(t):
                dve.wait_ge(S["up_done"], t + 1)
                dve.tensor_tensor(out=p1[:, :], in0=pu[:, 0:G], in1=b1_bc[:, :], op=ALU.add
                                  ).then_inc(S["p1_ready"], 1)
                dve.tensor_tensor(out=p2[:, :], in0=pu[:, G:2 * G], in1=b2_bc[:, :], op=ALU.add
                                  ).then_inc(S["pu_free"], 1)
                dve.wait_ge(S["th_ready"], t + 1)
                order.done(dve.scalar_tensor_tensor(out=p1[:, :], in0=th[:, :], scalar=1.0, in1=p1[:, :],
                                                    op0=ALU.add, op1=ALU.mult))
                order.wait()
                dve.wait_ge(S["pu_free"], t + 1)
                order.done(dve.tensor_tensor(out=p1[:, :], in0=p1[:, :], in1=p2[:, :], op=ALU.mult))
                order.wait()
                dve.tensor_tensor(out=p1[:, :].rearrange("p (e h) -> p e h", h=H),
                                  in0=p1[:, :].rearrange("p (e h) -> p e h", h=H),
                                  in1=x_w[:, :].unsqueeze(2).to_broadcast([P, NX, H]), op=ALU.mult
                                  ).then_inc(S["glu_ready"], 1)

            def output(t, u, turn):
                dve.wait_ge(S["d_done"], t + 1)
                dve.wait_ge(stored[u], 16 * turn)
                dve.tensor_tensor(out=out_t[:, u, :], in0=dp[:, :], in1=x1[:, u, :], op=ALU.add
                                  ).then_inc(S["out_ready"], 1)

            dve.wait_ge(S["acc_added"], 16 * CH)
            order.done(dve.memset(x_w_hl[:, :].bitcast(f32), 0.0))
            order.done(dve.memset(x_w[:, NE:NX], 0.5 / NS))
            order.wait()
            front(0, 0, 0)
            xnT(0)
            for k in range(KG):
                dve.wait_ge(S["dnhi_ready"], k + 1)
                dve.tensor_tensor(out=dn_lo[:, k, :], in0=out_t[:, k % 3, :],
                                  in1=dn_hi[:, k, :].bitcast(f32), op=ALU.subtract).then_inc(S["dn_ready"], 1)
            dve.wait_ge(S["obhi_ready"], 1)
            dve.scalar_tensor_tensor(out=ob_hl[32:KB, :], in0=ob_raw[32:KB, :], scalar=2.0,
                                     in1=ob_hl[32:KB, :].bitcast(f32), op0=ALU.mult, op1=ALU.subtract
                                     ).then_inc(S["dn_ready"], 1)
            dve.wait_ge(S["const_ready"], 4)

            def step(t, u, turn):
                last = isinstance(t, int) and t == TL - 1
                first = isinstance(t, int) and t == 0
                if not first:
                    gT(t - 1)
                if not last:
                    front(t + 1, (u + 1) % 3, turn + (u + 1) // 3)
                route(t)
                glu(t)
                if not last:
                    xnT(t + 1)
                if not first:
                    output(t - 1, (u - 1) % 3, turn + (u - 1) // 3)

            for t in range(4):
                step(t, t % 3, t // 3)
            with dve.Fori(0, (TL - 7) // 3) as j:
                order.enter(j, 3 * NODE_STEPS)
                for v in range(4, 7):
                    step(j * 3 + v, v % 3, j + v // 3)
            order.leave((TL - 7) // 3)
            for t in range(TL - 3, TL):
                step(t, t % 3, t // 3)
            gT(TL - 1)
            output(TL - 1, (TL - 1) % 3, (TL - 1) // 3)

        @block.tensor
        def _(pe):
            def product(out_ap, hi, lo, w_hi_ap, w_lo_ap, start, end, first, last):
                pieces = [(c, min(c + HALF, end)) for c in range(start, end, HALF)]
                for left, right, s, e in ((hi, w_hi_ap, first, False), (hi, w_lo_ap, False, False),
                                          (lo, w_hi_ap, False, last)):
                    for c0, c1 in pieces:
                        mm = pe.matmul(out_ap[:, c0:c1], left, right[:, c0:c1], start=s, stop=e)
                return mm

            pe.wait_ge(S["const_ready"], 3)
            pe.wait_ge(S["u_cols"], 1)
            for l in range(2):
                for k in range(KD):
                    last = pe.matmul(hp[l][:, k * P:(k + 1) * P], u_col[:, l, k:k + 1].to_broadcast([P, P]),
                                     ident[:, :], start=True, stop=True)
                last.then_inc(S["u_ps"], 1)

            def aggregate(k, s):
                pe.wait_ge(S["split_ready"], k + 1)
                for d in range(KD):
                    for part in (x_hi, x_lo):
                        pe.matmul(agg[:, d * P:(d + 1) * P], part[:, d * P:(d + 1) * P], same[:, s, :],
                                  start=part is x_hi, stop=part is x_lo)
                pe.matmul(e_sum[:, 0:1], same[:, s, :].bitcast(f32), e_w[:, s, :], start=True, stop=True
                          ).then_inc(S["agg_done"], 1)

            def times_w(k, s):
                pe.wait_ge(S["agglo_ready"], k + 1)
                pe.wait_ge(S["hp_free"], k + 1)
                for d in range(KD):
                    mm = product(hp[s], aggT_hi[:, s, d, :], aggT_lo[:, s, d, :], w_hi[:, d, :],
                                 w_lo[:, d, :], 0, D, d == 0, d == KD - 1)
                mm.then_inc(S["wmm_done"], 1)

            aggregate(0, 0)
            pe.wait_ge(S["w_split"], KD)
            with pe.Fori(0, CH // 2) as j:
                for s in range(2):
                    aggregate(j * 2 + (s + 1), 1 - s)
                    times_w(j * 2 + s, s)
            times_w(CH - 1, 0)

            def transpose_xn(t):
                pe.wait_ge(S["xn_ready"], t + 1)
                if not isinstance(t, int) or t >= 2:
                    pe.wait_ge(S["glo_ready"], t - 1)
                for d in range(KD):
                    last = pe.transpose(tp[:, d * P:(d + 1) * P], xn[:, d * P:(d + 1) * P], ident[:, :])
                last.then_inc(S["t_done"], 1)

            def expert_up(t):
                pe.wait_ge(S["xlo_n"], t + 1)
                pe.wait_ge(S["pu_free"], t)
                for d in range(KD):
                    mm = product(pu, xnT_hi[:, d, :], xnT_lo[:, d, :], up_hi[:, d * UP:(d + 1) * UP],
                                 up_lo[:, d * UP:(d + 1) * UP], 2 * HALF, UP, d == 0, d == KD - 1)
                mm.then_inc(S["gate_done"], 1)
                for d in range(KD):
                    mm = product(pu, xnT_hi[:, d, :], xnT_lo[:, d, :], up_hi[:, d * UP:(d + 1) * UP],
                                 up_lo[:, d * UP:(d + 1) * UP], 0, 2 * HALF, d == 0, d == KD - 1)
                mm.then_inc(S["up_done"], 1)

            def transpose_glu(t):
                pe.wait_ge(S["glu_ready"], t + 1)
                if isinstance(t, int) and t == TL - 1:
                    pass
                else:
                    pe.wait_ge(S["xlo_n"], t + 2)
                for g in range(KG):
                    pe.transpose(tp[:, g * P:(g + 1) * P], p1[:, g * P:(g + 1) * P], ident[:, :])
                pe.transpose(tp[0:KB, G:G + P], x_w_hl[:, :].bitcast(f32), ident[:, :]
                             ).then_inc(S["v_done"], 1)

            def expert_down(t):
                pe.wait_ge(S["glo_ready"], t + 1)
                pe.wait_ge(S["out_ready"], t)
                for g in range(KG):
                    product(dp, gT_hi[:, g, :], gT_lo[:, g, :], dn_hi[:, g, :], dn_lo[:, g, :],
                            0, D, g == 0, False)
                for c in range(2):
                    mm = pe.matmul(dp[:, c * HALF:(c + 1) * HALF], wT[:, :],
                                   ob_hl[:, c * HALF:(c + 1) * HALF], start=False, stop=True)
                mm.then_inc(S["d_done"], 1)

            transpose_xn(0)
            expert_up(0)
            transpose_xn(1)
            transpose_glu(0)
            pe.wait_ge(S["dn_ready"], KG + 1)

            def step(t):
                expert_up(t)
                if not isinstance(t, int) or t < TL - 1:
                    transpose_xn(t + 1)
                expert_down(t - 1)
                transpose_glu(t)

            step(1)
            with pe.Fori(2, TL - 1) as t:
                step(t)
            step(TL - 1)
            expert_down(TL - 1)





def kernel(x, src, dst, L0_gnn_W, L0_gnn_a, L0_ffn_gate_w, L0_ffn_gate_b, L0_ffn_rw1, L0_ffn_rb1,
           L0_ffn_rw2, L0_ffn_rb2, L0_ffn_rw3, L0_ffn_rb3, L0_ffn_sw1, L0_ffn_sb1, L0_ffn_sw2,
           L0_ffn_sb2, L0_ffn_sw3, L0_ffn_sb3):
    import numpy as np
    import concourse.bacc as bacc
    from concourse.bass_utils import run_bass_kernel_spmd

    def columns(w1):
        return np.asarray(w1).transpose(1, 0, 2).reshape(D, -1)

    idx = np.zeros((CH * P, 4), np.int32)
    idx[:, 0] = N
    idx[:E, 0] = np.asarray(src)
    idx[:E, 1] = np.asarray(src)
    idx[:E, 2] = np.asarray(dst)
    idx[:, 3] = np.arange(CH * P)
    up = np.concatenate([columns(L0_ffn_rw1), columns(L0_ffn_sw1), columns(L0_ffn_rw2),
                         columns(L0_ffn_sw2), np.asarray(L0_ffn_gate_w)], axis=1)
    up = up.reshape(KD, P, UP).transpose(1, 0, 2).reshape(P, -1)
    up = np.concatenate([up, np.zeros((P, UPN * UPW - up.shape[1]), np.float32)], axis=1)
    ins = {
        "x": np.asarray(x), "idx": idx, "keys": idx[:, 0], "where0": np.full(N + 16, SKIP, np.int32), "w": np.asarray(L0_gnn_W), "a": np.asarray(L0_gnn_a),
        "up": up, "gate_b": np.asarray(L0_ffn_gate_b),
        "b1": np.concatenate([np.asarray(L0_ffn_rb1).ravel(), np.asarray(L0_ffn_sb1).ravel()]),
        "b2": np.concatenate([np.asarray(L0_ffn_rb2).ravel(), np.asarray(L0_ffn_sb2).ravel()]),
        "dn": np.concatenate([np.asarray(L0_ffn_rw3).reshape(-1, D), np.asarray(L0_ffn_sw3).reshape(-1, D)]),
        "ob": np.concatenate([np.asarray(L0_ffn_rb3), np.asarray(L0_ffn_sb3)]),
    }
    nc = bacc.Bacc("TRN2", target_bir_lowering=False, num_devices=1)
    arrays, aps = {}, []
    for name, value in ins.items():
        value = np.ascontiguousarray(value)
        arrays[f"in_{name}"] = value
        aps.append(nc.dram_tensor(f"in_{name}", value.shape, mybir.dt.from_np(value.dtype),
                                  kind="ExternalInput").ap())
    aps.append(nc.dram_tensor("out_0", (N, D), mybir.dt.float32, kind="ExternalOutput").ap())
    build(nc, *aps)
    return run_bass_kernel_spmd(nc, [arrays], core_ids=[0]).results[0]["out_0"]
```

```python
import concourse.bass as bass
from concourse import mybir
from contextlib import ExitStack

N = 10000
E = 10000
D = 1024
NE, NS, H = 8, 2, 64
NX = NE + NS
G = NX * H
P = 128
KD = D // P
KG = G // P
UP = 2 * G + NE
CH = -(-E // P)
TL = -(-N // P)
ROW = D + 16
SKIP = 16384
UPN = (CH - 3) // 2
UPW = 2 * -(-KD * UP // (2 * UPN))
SLOPE = 0.1
EPS_ROW = 1e-5
EPS_LN = 1e-5
KB = 64
HALF = D // 2
EDGE_STEPS = 10
NODE_STEPS = 19
POOL_K = (0, 2, 4, 6)
DVE_SLICES = [sum(1 if j in POOL_K else 2 for j in range(k + 1)) for k in range(KD)]


class Order:

    def __init__(self, eng, sem):
        self.eng, self.sem, self.base, self.n = eng, sem, 0, 0

    def done(self, instruction):
        instruction.then_inc(self.sem, 1)
        self.n += 1
        return instruction

    def wait(self, but=0):
        self.eng.wait_ge(self.sem, self.base + self.n - but)

    def enter(self, j, steps):
        self.before, self.steps = self.base + self.n, steps
        self.base, self.n = self.before + j * steps, 0

    def leave(self, turns):
        assert self.n == self.steps, (self.n, self.steps)
        self.base, self.n = self.before + turns * self.steps, 0


def build(nc, x, idx, keys, where0, w, a, up, gate_b, b1, b2, dn, ob, out):
    f32, f32r, i32, bf16 = mybir.dt.float32, mybir.dt.float32r, mybir.dt.int32, mybir.dt.bfloat16
    ALU = mybir.AluOpType
    ACT = mybir.ActivationFunctionType
    AX = mybir.AxisListType.X

    acc = nc.dram_tensor("acc", [CH * P, ROW], f32).ap()
    where = nc.dram_tensor("where", [N + 16, 1], i32).ap()
    w_rows = w.rearrange("(k p) n -> p k n", p=P)
    dn_rows = dn.rearrange("(k p) n -> p k n", p=P)

    whole, edges, nodes = ExitStack(), ExitStack(), ExitStack()
    with whole:
        def sem(name):
            return whole.enter_context(nc.semaphore(name))

        def tile(stack, name, shape, dt=f32):
            return stack.enter_context(nc.sbuf_tensor(name, shape, dt))

        def bank(stack, name, shape):
            return stack.enter_context(nc.psum_tensor(name, shape, f32))

        ident = tile(whole, "ident", [P, P])
        below = tile(whole, "below", [P, P])
        with ExitStack() as staging:
            w_raw = tile(staging, "w_raw", [P, KD, D])
            a_bc = tile(staging, "a_bc", [P, 2, D])
        up_hi = tile(whole, "up_hi", [P, UPN * UPW], f32r)
        up_lo = tile(whole, "up_lo", [P, UPN * UPW], f32r)
        minus_half = tile(whole, "minus_half", [P, 2])
        where_t = [tile(whole, f"where_t{u}", [P, 1], i32) for u in range(3)]
        stats = tile(whole, "stats", [P, 2, 12])
        mean_var = tile(whole, "mean_var", [P, 2, 2])
        var_eps = tile(whole, "var_eps", [P, 2])
        rstd = tile(whole, "rstd", [P, 2])
        affine = tile(whole, "affine", [P, 2])

        with edges:
            src_rows = tile(edges, "src_rows", [P, 2, D])
            dst_rows = tile(edges, "dst_rows", [P, 2, D])
            x_hi = tile(edges, "x_hi", [P, D], f32r)
            x_lo = tile(edges, "x_lo", [P, D], f32r)
            u_bc = tile(edges, "u_bc", [P, 2, D])
            junk = tile(edges, "junk", [P, D], bf16)
            w_hi = tile(edges, "w_hi", [P, KD, D], f32r)
            w_lo = tile(edges, "w_lo", [P, KD, D], f32r)
            u_col = tile(edges, "u_col", [P, 2, KD])
            u_sum = tile(edges, "u_sum", [P, 2])
            up_raw = tile(edges, "up_raw", [P, UPW])
            result = tile(edges, "result", [P, 2, ROW])
            same = tile(edges, "same", [P, 2, P], f32r)
            aggT_hi = tile(edges, "aggT_hi", [P, 2, KD, P], f32r)
            aggT_lo = tile(edges, "aggT_lo", [P, 2, KD, P], f32r)
            edge_idx = [tile(edges, f"edge_idx{s}", [P, 4], i32) for s in range(2)]
            src_keys = tile(edges, "src_keys", [P, 2, P], i32)
            add_idx = [tile(edges, f"add_idx{s}", [P, 1], i32) for s in range(2)]
            first_idx = [tile(edges, f"first_idx{s}", [P, 1], i32) for s in range(2)]
            edge_no = [tile(edges, f"edge_no{s}", [P, 1], i32) for s in range(2)]
            where_e = [tile(edges, f"where_e{s}", [P, 1], i32) for s in range(2)]
            of_edge = tile(edges, "of_edge", [P, 8])
            src_key, earlier, logit, skip, first_row, e_w = (of_edge[:, c:c + 1] for c in range(6))
            dots = of_edge[:, 6:8]
            mean_u = tile(edges, "mean_u", [P, 2])
            e_hl = tile(edges, "e_hl", [P, 2], f32r)
            add_row = tile(edges, "add_row", [P, 2, 1])
            sum_row = tile(edges, "sum_row", [P, 2, 2])
            with ExitStack() as banks:
                agg = bank(banks, "agg", [P, D])
                hp = [bank(banks, f"hp{s}", [P, D]) for s in range(2)]
                e_sum = bank(banks, "e_sum", [P, HALF])

        with nodes:
            acc_t = tile(nodes, "acc_t", [P, 3, ROW])
            x1 = tile(nodes, "x1", [P, 3, D])
            b1_bc = tile(nodes, "b1_bc", [P, G])
            b2_bc = tile(nodes, "b2_bc", [P, G])
            ob_raw = tile(nodes, "ob_raw", [KB, D])
            gb_bc = tile(nodes, "gb_bc", [P, NE])
            before = tile(nodes, "before", [P, NE, NE])
            dn_hi = tile(nodes, "dn_hi", [P, KG, D], f32r)
            dn_lo = tile(nodes, "dn_lo", [P, KG, D], f32r)
            ob_hl = tile(nodes, "ob_hl", [KB, D], f32r)
            out_t = tile(nodes, "out_t", [P, 3, D])
            exp_y = tile(nodes, "exp_y", [P, D])
            xn = tile(nodes, "xn", [P, D])
            xnT_hi = tile(nodes, "xnT_hi", [P, KD, P], f32r)
            xnT_lo = tile(nodes, "xnT_lo", [P, KD, P], f32r)
            p1 = tile(nodes, "p1", [P, G])
            p2 = tile(nodes, "p2", [P, G])
            th = tile(nodes, "th", [P, G])
            gT_hi = tile(nodes, "gT_hi", [P, KG, P], f32r)
            gT_lo = tile(nodes, "gT_lo", [P, KG, P], f32r)
            wT = tile(nodes, "wT", [KB, P], f32r)
            den = tile(nodes, "den", [P, 3])
            lg = tile(nodes, "lg", [P, NE])
            greater = tile(nodes, "greater", [P, NE, NE])
            equal = tile(nodes, "equal", [P, NE, NE])
            rank = tile(nodes, "rank", [P, NE])
            neg_max = tile(nodes, "neg_max", [P, 1])
            exp_l = tile(nodes, "exp_l", [P, NE])
            exp_sum = tile(nodes, "exp_sum", [P, 2])
            x_w = tile(nodes, "x_w", [P, NX])
            x_w_hl = tile(nodes, "x_w_hl", [P, KB], f32r)
            with ExitStack() as banks:
                tp = bank(banks, "tp", [P, D])
                pu = bank(banks, "pu", [P, 3 * HALF])
                dp = bank(banks, "dp", [P, D])

        names = """const_ready a_loaded w_split u_part wa_ready u_ps u_bc_ready
            split_ready agglo_ready agghi_ready agg_done wmm_done hp_free result_ready res_free
            acc_added where_begun where_read where_written first_ready idx_used up_loaded up_split uphi_ready
            var_ready rstd_ready logit_ready e_ready scale_ready xhi_ready
            dnhi_ready dn_ready consts_loaded ob_zero rinv_ready expy_ready norm_ready xn_ready
            t_done xhi_n xlo_n gate_done up_done pu_free p1_ready th_ready glu_ready v_done
            ghi_ready glo_ready d_done out_ready lmax_ready expl_ready
            stats_done gathers_begun whi_ready obhi_ready
            vector_step scalar_step pool_step""".split()
        S = {n: sem(n) for n in names}
        w_loaded = [sem(f"w_loaded{i}") for i in range(KD)]
        dn_loaded = [sem(f"dn_loaded{i}") for i in range(3)]
        idx_loaded = [sem(f"idx_loaded{i}") for i in range(2)]
        gathered = [sem(f"gathered{i}") for i in range(2)]
        rows_stored = [sem(f"rows_stored{i}") for i in range(2)]
        x_loaded = [sem(f"x_loaded{i}") for i in range(3)]
        where_loaded = [sem(f"where_loaded{i}") for i in range(3)]
        acc_loaded = [sem(f"acc_loaded{i}") for i in range(3)]
        stored = [sem(f"stored{i}") for i in range(3)]
        block = whole.enter_context(nc.Block())

        def row0(t):
            return N - P if isinstance(t, int) and t == TL - 1 else t * P

        @block.sync
        def _(sp):
            def load_indices(k, s):
                sp.dma_start(edge_idx[s][:, :], idx[bass.ds(k * P, P), :]).then_inc(idx_loaded[s], 16)
                sp.dma_start(src_keys[:, s, :],
                             keys[bass.ds(k * P, P)].partition_broadcast(P)
                             ).then_inc(idx_loaded[s], 16)

            def store_rows(k, s):
                sp.wait_ge(S["result_ready"], k + 1)
                sp.dma_start(acc[bass.ds(k * P, P), :], result[:, s, :]).then_inc(rows_stored[s], 16)

            load_indices(0, 0)
            for k in range(KD):
                if k < 2:
                    sp.dma_start(a_bc[:, k, :], a[0, k * D:(k + 1) * D].partition_broadcast(P)
                                 ).then_inc(S["a_loaded"], 16)
                sp.dma_start(w_raw[:, k, :], w_rows[:, k, :]).then_inc(w_loaded[k], 16)
            load_indices(1, 1)
            sp.dma_start(where.rearrange("(a b) o -> a (b o)", a=16), where0.rearrange("(a b) -> a b", a=16)
                         ).then_inc(S["where_begun"], 16)
            sp.wait_ge(S["idx_used"], 1)
            load_indices(2, 0)
            sp.wait_ge(S["idx_used"], 2)
            load_indices(3, 1)
            with sp.Fori(0, UPN - 1) as j:
                sp.wait_ge(S["up_split"], j + 1)
                sp.dma_start(up_raw[:, :], up[:, bass.ds(j * UPW, UPW)]).then_inc(S["up_loaded"], 16)
                for s in range(2):
                    sp.wait_ge(S["idx_used"], j * 2 + (s + 3))
                    load_indices(j * 2 + (s + 4), s)
                    store_rows(j * 2 + s, s)
            sp.wait_ge(S["up_split"], UPN)
            sp.dma_start(up_raw[:, :], up[:, (UPN - 1) * UPW:]).then_inc(S["up_loaded"], 16)
            sp.wait_ge(S["idx_used"], CH - 2)
            load_indices(CH - 1, (CH - 1) % 2)
            for k in range(CH - 5, CH - 2):
                store_rows(k, k % 2)

            def load_x(t, u):
                sp.dma_start(x1[:, u, :], x[bass.ds(row0(t), P), :]).then_inc(x_loaded[u], 16)

            def load_where(t, u):
                sp.dma_start(where_t[u][:, :], where[bass.ds(row0(t), P), :]).then_inc(where_loaded[u], 16)

            def store_tile(t, u):
                if isinstance(t, int) and t == TL - 1:
                    new = N - (TL - 1) * P
                    sp.dma_start(out[N - new:N, :], out_t[P - new:P, u, :]).then_inc(stored[u], 16)
                else:
                    sp.dma_start(out[bass.ds(row0(t), P), :], out_t[:, u, :]).then_inc(stored[u], 16)

            sp.wait_ge(S["where_written"], 16 * CH)
            for t in range(3):
                load_where(t, t)
            sp.wait_ge(S["agg_done"], CH)
            sp.dma_start(gb_bc[:, :], gate_b.partition_broadcast(P)).then_inc(S["consts_loaded"], 16)
            for t in range(3):
                load_x(t, t)
            sp.dma_start(b1_bc[:, :], b1.partition_broadcast(P)).then_inc(S["consts_loaded"], 16)
            sp.dma_start(b2_bc[:, :], b2.partition_broadcast(P)).then_inc(S["consts_loaded"], 16)
            sp.wait_ge(S["ob_zero"], 1)
            for r in (0, NX, 32, 32 + NX):
                sp.dma_start(ob_raw[r:r + NX, :], ob).then_inc(S["consts_loaded"], 16)
            for k in range(CH - 2, CH):
                store_rows(k, k % 2)
            sp.wait_ge(rows_stored[0], 16 * (CH - CH // 2))
            sp.wait_ge(rows_stored[1], 16 * (CH // 2))
            sp.wait_ge(S["acc_added"], 16 * CH)
            sp.wait_ge(acc_loaded[0], 16)
            for k in range(KG):
                if k >= 3:
                    sp.wait_ge(S["dn_ready"], k - 2)
                sp.dma_start(out_t[:, k % 3, :], dn_rows[:, k, :]).then_inc(dn_loaded[k % 3], 16)
            sp.wait_ge(S["norm_ready"], 1)
            load_where(3, 0)
            with sp.Fori(0, (TL - 7) // 3) as j:
                for u in range(3):
                    sp.wait_ge(S["out_ready"], j * 3 + u + 1)
                    load_x(j * 3 + (u + 3), u)
                    load_where(j * 3 + (u + 4), (u + 1) % 3)
                    store_tile(j * 3 + u, u)
            for t in range(TL - 7, TL):
                sp.wait_ge(S["out_ready"], t + 1)
                if t + 3 < TL:
                    load_x(t + 3, t % 3)
                if t + 4 < TL:
                    load_where(t + 4, (t + 1) % 3)
                store_tile(t, t % 3)
            for u in range(3):
                sp.wait_ge(stored[u], 16 * len(range(u, TL, 3)))

        @block.gpsimd
        def _(pool):
            order = Order(pool, S["pool_step"])
            order.done(pool.memset(ident[:, :], 0.0))
            order.done(pool.memset(below[:, :], 1.0))
            pool.memset(minus_half[:, :], -0.5).then_inc(S["const_ready"], 1)
            order.wait()
            pool.affine_select(out=ident[:, :], in_=ident[:, :], compare_op=ALU.not_equal, fill=1.0,
                               base=0, pattern=[[-1, P]], channel_multiplier=1).then_inc(S["const_ready"], 1)
            pool.affine_select(out=below[:, :], in_=below[:, :], compare_op=ALU.is_gt, fill=0.0,
                               base=0, pattern=[[-1, P]], channel_multiplier=1).then_inc(S["const_ready"], 1)
            def gather(k, s, turn):
                pool.wait_ge(idx_loaded[s], 32 * (turn + 1))
                pool.sem_inc(S["gathers_begun"], 1)
                for rows, col in ((src_rows, 1), (dst_rows, 2)):
                    pool.indirect_dma_start(
                        out=rows[:, s, :], out_offset=None, in_=x,
                        in_offset=bass.IndirectOffsetOnAxis(ap=edge_idx[s][:, col:col + 1], axis=0)
                        ).then_inc(gathered[s], 16)

            def power(k):
                pool.wait_ge(S["var_ready"], k + 1)
                pool.tensor_tensor(out=rstd[:, :], in0=var_eps[:, :], in1=minus_half[:, :],
                                   op=ALU.pow).then_inc(S["rstd_ready"], 1)

            def read_where(k, s, turn):
                pool.wait_ge(idx_loaded[s], 32 * (turn + 1))
                if isinstance(k, int) and k == 0:
                    pool.wait_ge(S["where_begun"], 16)
                else:
                    pool.wait_ge(S["where_written"], k * 16)
                pool.sem_inc(S["gathers_begun"], 1)
                pool.indirect_dma_start(
                    out=where_e[s][:, :], out_offset=None, in_=where,
                    in_offset=bass.IndirectOffsetOnAxis(ap=edge_idx[s][:, 0:1], axis=0)
                    ).then_inc(S["where_read"], 16)

            def write_where(k, s):
                pool.wait_ge(S["first_ready"], k + 1)
                pool.wait_ge(S["where_read"], (k + 1) * 16)
                pool.sem_inc(S["idx_used"], 1)
                pool.indirect_dma_start(
                    out=where, out_offset=bass.IndirectOffsetOnAxis(ap=first_idx[s][:, :], axis=0),
                    in_=edge_no[s][:, :], in_offset=None, bounds_check=N - 1, oob_is_err=False
                    ).then_inc(S["where_written"], 16)

            def add_rows(k, s, turn):
                n = E - k * P if isinstance(k, int) and k == CH - 1 else P
                pool.wait_ge(S["result_ready"], k + 1)
                if not isinstance(k, int) or k > 0:
                    pool.wait_ge(rows_stored[1 - s], (turn + 1) * 16)
                    pool.wait_ge(S["acc_added"], k * 16)
                pool.sem_inc(S["res_free"], 1)
                pool.indirect_dma_start(
                    out=acc, out_offset=bass.IndirectOffsetOnAxis(ap=add_idx[s][0:n, :], axis=0),
                    in_=result[0:n, s, :], in_offset=None, bounds_check=CH * P - 1, oob_is_err=False,
                    compute_op=ALU.add).then_inc(S["acc_added"], 16)

            pool.sem_inc(S["res_free"], 1)
            pool.wait_ge(S["a_loaded"], 32)
            for i, k in enumerate(POOL_K):
                pool.wait_ge(w_loaded[k], 16)
                if i >= 2:
                    pool.wait_ge(S["u_part"], i - 1)
                pool.tensor_tensor(out=result[:, i % 2, 0:D], in0=w_raw[:, k, :], in1=a_bc[:, 1, :],
                                   op=ALU.mult).then_inc(S["wa_ready"], 1)
            gather(0, 0, 0)
            gather(1, 1, 0)
            read_where(0, 0, 0)
            power(0)
            write_where(0, 0)

            def edge_step(p, s, turn):
                pool.wait_ge(S["split_ready"], p + 1)
                read_where(p + 1, 1 - s, turn + s)
                power(p + 1)
                if not isinstance(p, int) or p + 2 < CH:
                    gather(p + 2, s, turn + 1)
                if not isinstance(p, int) or p >= 2:
                    add_rows(p - 2, s, turn - 1 - (1 - s))
                write_where(p + 1, 1 - s)

            for p in range(4):
                edge_step(p, p % 2, p // 2)
            with pool.Fori(0, (CH - 7) // 2) as j:
                for s in range(2):
                    edge_step(j * 2 + (s + 4), s, j + 2)
            for p in range(CH - 3, CH - 1):
                edge_step(p, p % 2, p // 2)
            add_rows(CH - 3, 0, (CH - 4) // 2)
            pool.wait_ge(S["agg_done"], CH)
            pool.memset(ob_raw[:, :], 0.0).then_inc(S["ob_zero"], 1)
            order.done(pool.memset(acc_t[:, :, :], 0.0))
            order.done(pool.memset(before[:, :, :], 1.0))
            order.wait()
            pool.affine_select(out=before[:, :, :], in_=before[:, :, :], compare_op=ALU.is_gt, fill=0.0,
                               base=0, pattern=[[1, NE], [-1, NE]], channel_multiplier=0
                               ).then_inc(S["const_ready"], 1)
            for k in range(CH - 2, CH):
                add_rows(k, k % 2, (k - 1) // 2)
            pool.wait_ge(S["acc_added"], 16 * CH)
            pool.wait_ge(rows_stored[(CH - 1) % 2], 16 * (CH - CH // 2))

            def gather_acc(t, u, turn):
                pool.wait_ge(where_loaded[u], (turn + 1) * 16)
                pool.sem_inc(S["gathers_begun"], 1)
                pool.indirect_dma_start(
                    out=acc_t[:, u, :], out_offset=None, in_=acc,
                    in_offset=bass.IndirectOffsetOnAxis(ap=where_t[u][:, :], axis=0),
                    bounds_check=CH * P - 1, oob_is_err=False).then_inc(acc_loaded[u], 16)

            for t in range(3):
                gather_acc(t, t, 0)
            power(CH)
            power(CH + 1)
            with pool.Fori(0, (TL - 4) // 3) as j:
                for u in range(3):
                    pool.wait_ge(S["norm_ready"], j * 3 + (u + 1))
                    gather_acc(j * 3 + (u + 3), u, j + 1)
                    power(j * 3 + (u + 2 + CH))
            gather_acc(TL - 1, (TL - 1) % 3, (TL - 1) // 3)
            for t in range(TL - 2, TL):
                power(CH + t)

        @block.scalar
        def _(act):
            order = Order(act, S["scalar_step"])
            act.wait_ge(S["const_ready"], 3)
            def sum_part(i):
                act.wait_ge(S["wa_ready"], i + 1)
                act.activation(result[:, i % 2, 0:D], result[:, i % 2, 0:D], ACT.Copy,
                               accum_out=u_col[:, 1, POOL_K[i]:POOL_K[i] + 1]).then_inc(S["u_part"], 1)

            for k in range(KD):
                act.wait_ge(w_loaded[k], 16)
                act.activation(w_hi[:, k, :], w_raw[:, k, :], ACT.Copy).then_inc(S["whi_ready"], 1)
                if k - 2 in POOL_K:
                    sum_part(POOL_K.index(k - 2))
            for i, k in enumerate(POOL_K):
                if k + 2 >= KD:
                    sum_part(i)
            act.wait_ge(S["u_ps"], 1)
            for l in range(2):
                act.activation(u_bc[:, l, :], hp[l][:, :], ACT.Copy, accum_out=u_sum[:, l:l + 1]
                               ).then_inc(S["u_bc_ready"], 1)
            act.wait_ge(S["u_bc_ready"], 2)
            act.sem_inc(S["hp_free"], 2)

            def edge_rows(k, s):
                act.wait_ge(S["logit_ready"], k + 1)
                act.activation(e_w[:, :], logit[:, :], ACT.Exp, scale=-1.0).then_inc(S["e_ready"], 1)
                act.wait_ge(S["scale_ready"], k + 1)
                order.done(act.activation(dst_rows[:, s, :], dst_rows[:, s, :], ACT.Identity,
                                          scale=affine[:, 0:1], bias=affine[:, 1:2]))
                act.activation(e_hl[:, 0:1], e_w[:, :], ACT.Copy)
                order.wait()
                act.activation(x_hi[:, :], dst_rows[:, s, :], ACT.Copy).then_inc(S["xhi_ready"], 1)

            def agg_hi(k, s):
                act.wait_ge(S["agg_done"], k + 1)
                act.activation(aggT_hi[:, s, :, :].rearrange("p k e -> p (k e)"), agg[:, :], ACT.Copy
                               ).then_inc(S["agghi_ready"], 1)

            def evacuate(k, s):
                act.wait_ge(S["wmm_done"], k + 1)
                act.wait_ge(S["res_free"], k + 1)
                act.activation(result[:, s, 0:D], hp[s][:, :], ACT.Copy).then_inc(S["hp_free"], 1)
                act.activation(result[:, s, D:D + 1], sum_row[:, s, 0:1], ACT.Copy)
                act.activation(add_idx[s][:, :], sum_row[:, s, 1:2], ACT.Copy).then_inc(S["result_ready"], 1)

            def edge_step(p, s):
                if not isinstance(p, int) or p >= 2:
                    evacuate(p - 2, s)
                agg_hi(p, s)
                if not isinstance(p, int) or p + 1 < CH:
                    edge_rows(p + 1, 1 - s)

            edge_rows(0, 0)
            edge_step(0, 0)
            edge_step(1, 1)
            with act.Fori(0, UPN) as j:
                order.enter(j, 2)
                act.wait_ge(S["up_loaded"], (j + 1) * 16)
                act.wait_ge(S["up_split"], j + 1)
                act.activation(up_hi[:, bass.ds(j * UPW, UPW)], up_raw[:, :], ACT.Copy
                               ).then_inc(S["uphi_ready"], 1)
                for s in range(2):
                    edge_step(j * 2 + (s + 2), s)
            order.leave(UPN)
            edge_step(CH - 1, 0)
            evacuate(CH - 2, 1)
            evacuate(CH - 1, 0)

            def front(t, u):
                act.wait_ge(S["rinv_ready"], t + 1)
                act.activation(exp_y[:, :], acc_t[:, u, 0:D], ACT.Exp, scale=den[:, 2:3]
                               ).then_inc(S["expy_ready"], 1)
                act.wait_ge(S["norm_ready"], t + 1)
                act.activation(xn[:, :], x1[:, u, :], ACT.Identity, scale=affine[:, 0:1],
                               bias=affine[:, 1:2]).then_inc(S["xn_ready"], 1)

            def xnT(t):
                act.wait_ge(S["t_done"], t + 1)
                act.activation(xnT_hi[:, :, :].rearrange("p k e -> p (k e)"), tp[:, :], ACT.Copy
                               ).then_inc(S["xhi_n"], 1)

            def gT(t):
                act.wait_ge(S["v_done"], t + 1)
                act.activation(gT_hi[:, :, :].rearrange("p k e -> p (k e)"), tp[:, 0:G], ACT.Copy
                               ).then_inc(S["ghi_ready"], 1)

            def exp_logits(t):
                act.wait_ge(S["lmax_ready"], t + 1)
                act.activation(exp_l[:, :], lg[:, :], ACT.Exp, bias=neg_max[:, :],
                               accum_out=exp_sum[:, 0:1]).then_inc(S["expl_ready"], 1)

            def silu(t):
                act.wait_ge(S["p1_ready"], t + 1)
                act.activation(th[:, :], p1[:, :], ACT.Tanh, scale=0.5).then_inc(S["th_ready"], 1)

            front(0, 0)
            xnT(0)

            def dn_round(k):
                act.wait_ge(dn_loaded[k % 3], 16 * (k // 3 + 1))
                act.activation(dn_hi[:, k, :], out_t[:, k % 3, :], ACT.Copy).then_inc(S["dnhi_ready"], 1)

            for k in range(3):
                dn_round(k)
            front(1, 1)
            exp_logits(0)
            xnT(1)
            silu(0)
            for k in range(3, KG):
                dn_round(k)
            act.wait_ge(S["consts_loaded"], 16 * 7)
            act.activation(ob_hl[:, :], ob_raw[:, :], ACT.Copy, scale=2.0).then_inc(S["obhi_ready"], 1)

            def step(t, u):
                if isinstance(t, int) and t == 1:
                    front(t + 1, (u + 1) % 3)
                gT(t - 1)
                if not isinstance(t, int) or 1 < t < TL - 1:
                    front(t + 1, (u + 1) % 3)
                exp_logits(t)
                silu(t)
                if not isinstance(t, int) or t < TL - 1:
                    xnT(t + 1)

            for t in range(1, 4):
                step(t, t % 3)
            with act.Fori(0, (TL - 7) // 3) as j:
                for v in range(4, 7):
                    step(j * 3 + v, v % 3)
            for t in range(TL - 3, TL):
                step(t, t % 3)
            gT(TL - 1)

        @block.vector
        def _(dve):
            order = Order(dve, S["vector_step"])
            dve.memset(result[:, :, D:ROW], 0.0)
            dots_of_w = [(k, l) for k in range(KD) for l in range(2) if l == 0 or k not in POOL_K]
            for i, (k, l) in enumerate(dots_of_w):
                if i == 0:
                    dve.wait_ge(S["a_loaded"], 16)
                if l == 1:
                    dve.wait_ge(S["a_loaded"], 32)
                dve.wait_ge(w_loaded[k], 16)
                if i >= 2:
                    order.wait(1)
                place = (junk[:, :], u_bc[:, 0, :])[i % 2]
                order.done(dve.tensor_tensor_reduce(
                    out=place, in0=w_raw[:, k, :], in1=a_bc[:, l, :], scale=1.0, scalar=0.0,
                    op0=ALU.mult, op1=ALU.add, accum_out=u_col[:, l, k:k + 1]))
            order.wait()

            def w_split(k):
                dve.wait_ge(S["whi_ready"], k + 1)
                dve.tensor_tensor(out=w_lo[:, k, :], in0=w_raw[:, k, :],
                                  in1=w_hi[:, k, :].bitcast(f32), op=ALU.subtract).then_inc(S["w_split"], 1)

            def logits(k, s, turn):
                def dot(r):
                    order.done(dve.tensor_tensor_reduce(
                        out=junk[:, :], in0=(src_rows, dst_rows)[r][:, s, :], in1=u_bc[:, r, :],
                        scale=1.0, scalar=0.0, op0=ALU.mult, op1=ALU.add, accum_out=dots[:, r:r + 1]))

                dve.wait_ge(gathered[s], 32 * (turn + 1))
                for r, rows in enumerate((src_rows, dst_rows)):
                    for h in range(2):
                        last = dve.bn_stats(out=stats[:, r, 6 * h:6 * h + 6],
                                            in_=rows[:, s, h * HALF:(h + 1) * HALF])
                order.done(last)
                order.wait()
                dot(0)
                for r in range(2):
                    last = dve.bn_aggr(out=mean_var[:, r, :], in_=stats[:, r, :])
                order.done(last)
                order.wait()
                dve.tensor_scalar(out=var_eps[:, :], in0=mean_var[:, :, 1], scalar1=EPS_LN, scalar2=None,
                                  op0=ALU.add).then_inc(S["var_ready"], 1)
                dot(1)
                dve.tensor_tensor(out=mean_u[:, :], in0=mean_var[:, :, 0], in1=u_sum[:, :], op=ALU.mult)
                dve.wait_ge(idx_loaded[s], 32 * (turn + 1))
                dve.tensor_copy(edge_no[s][:, :], edge_idx[s][:, 3:4])
                order.done(dve.tensor_copy(src_key[:, :], edge_idx[s][:, 0:1]))
                order.wait()
                dve.tensor_tensor(out=dots[:, :], in0=dots[:, :], in1=mean_u[:, :], op=ALU.subtract)
                order.done(dve.tensor_scalar(out=same[:, s, :], in0=src_keys[:, s, :], scalar1=src_key[:, :],
                                             scalar2=None, op0=ALU.is_equal))
                order.wait()
                order.done(dve.tensor_tensor_reduce(out=junk[:, 0:P], in0=same[:, s, :].bitcast(f32),
                                                    in1=below[:, :], scale=1.0, scalar=0.0, op0=ALU.mult,
                                                    op1=ALU.add, accum_out=earlier[:, :]))
                dve.wait_ge(S["rstd_ready"], k + 1)
                order.done(dve.tensor_tensor_reduce(out=junk[:, P:P + 2], in0=dots[:, :], in1=rstd[:, :],
                                                    scale=1.0, scalar=0.0, op0=ALU.mult, op1=ALU.add,
                                                    accum_out=logit[:, :]))
                order.wait()
                dve.scalar_tensor_tensor(out=logit[:, :], in0=logit[:, :], scalar=SLOPE, in1=logit[:, :],
                                         op0=ALU.mult, op1=ALU.max).then_inc(S["logit_ready"], 1)
                dve.wait_ge(S["where_read"], (k + 1) * 16)
                dve.tensor_scalar(out=skip[:, :], in0=where_e[s][:, :], scalar1=float(SKIP),
                                  scalar2=float(SKIP), op0=ALU.is_lt, op1=ALU.mult)
                order.done(dve.scalar_tensor_tensor(
                    out=first_row[:, :], in0=earlier[:, :], scalar=float(SKIP), in1=src_key[:, :],
                    op0=ALU.mult, op1=ALU.add))
                dve.scalar_tensor_tensor(out=add_row[:, s, :], in0=earlier[:, :], scalar=float(SKIP),
                                         in1=where_e[s][:, :], op0=ALU.mult, op1=ALU.add)
                order.wait()
                dve.tensor_tensor(out=first_idx[s][:, :], in0=first_row[:, :], in1=skip[:, :], op=ALU.add
                                  ).then_inc(S["first_ready"], 1)
                dve.wait_ge(S["e_ready"], k + 1)
                order.done(dve.tensor_tensor(out=affine[:, 0:1], in0=e_w[:, :], in1=rstd[:, 1:2],
                                             op=ALU.mult))
                order.wait()
                dve.scalar_tensor_tensor(out=affine[:, 1:2], in0=mean_var[:, 1, 0:1], scalar=-1.0,
                                         in1=affine[:, 0:1], op0=ALU.mult, op1=ALU.mult
                                         ).then_inc(S["scale_ready"], 1)

            def x_split(k, s):
                dve.wait_ge(S["xhi_ready"], k + 1)
                dve.tensor_tensor(out=e_hl[:, 1:2], in0=e_w[:, :], in1=e_hl[:, 0:1].bitcast(f32),
                                  op=ALU.subtract)
                dve.tensor_tensor(out=x_lo[:, :], in0=dst_rows[:, s, :], in1=x_hi[:, :].bitcast(f32),
                                  op=ALU.subtract).then_inc(S["split_ready"], 1)

            def agg_lo(k, s):
                dve.wait_ge(S["agghi_ready"], k + 1)
                dve.tensor_reduce(out=sum_row[:, s, 0:1], in_=e_sum[:, 0:2], axis=AX, op=ALU.add)
                dve.tensor_copy(sum_row[:, s, 1:2], add_row[:, s, :])
                dve.tensor_tensor(out=aggT_lo[:, s, :, :].rearrange("p k e -> p (k e)"), in0=agg[:, :],
                                  in1=aggT_hi[:, s, :, :].rearrange("p k e -> p (k e)").bitcast(f32),
                                  op=ALU.subtract).then_inc(S["agglo_ready"], 1)

            def edge_step(p, s, turn):
                if not isinstance(p, int) or p + 1 < CH:
                    logits(p + 1, 1 - s, turn + s)
                agg_lo(p, s)
                if not isinstance(p, int) or p + 1 < CH:
                    x_split(p + 1, 1 - s)

            for k in range(0, 3):
                w_split(k)
            dve.wait_ge(S["u_bc_ready"], 2)
            logits(0, 0, 0)
            for k in range(3, 5):
                w_split(k)
            x_split(0, 0)
            logits(1, 1, 0)
            agg_lo(0, 0)
            w_split(5)
            x_split(1, 1)
            for k in range(6, KD):
                w_split(k)
            dve.wait_ge(S["w_split"], KD)
            dve.sem_inc(S["up_split"], 1)
            edge_step(1, 1, 0)
            with dve.Fori(0, UPN) as j:
                order.enter(j, 2 * EDGE_STEPS)
                dve.wait_ge(S["uphi_ready"], j + 1)
                dve.tensor_tensor(out=up_lo[:, bass.ds(j * UPW, UPW)], in0=up_raw[:, :],
                                  in1=up_hi[:, bass.ds(j * UPW, UPW)].bitcast(f32), op=ALU.subtract
                                  ).then_inc(S["up_split"], 1)
                for s in range(2):
                    edge_step(j * 2 + (s + 2), s, j + 1)
            order.leave(UPN)
            edge_step(CH - 1, 0, 0)

            def front(t, u, turn):
                dve.wait_ge(acc_loaded[u], 16 * (turn + 1))
                order.done(dve.tensor_scalar(out=den[:, 0:1], in0=acc_t[:, u, D:D + 1], scalar1=EPS_ROW,
                                             scalar2=None, op0=ALU.add))
                order.wait()
                order.done(dve.reciprocal(den[:, 1:2], den[:, 0:1]))
                order.wait()
                dve.scalar_tensor_tensor(out=den[:, 2:3], in0=where_t[u][:, :], scalar=float(SKIP),
                                         in1=den[:, 1:2], op0=ALU.is_lt, op1=ALU.mult
                                         ).then_inc(S["rinv_ready"], 1)
                dve.wait_ge(S["expy_ready"], t + 1)
                order.done(dve.tensor_scalar(out=exp_y[:, :], in0=exp_y[:, :], scalar1=1.0, scalar2=-1.0,
                                             op0=ALU.min, op1=ALU.add))
                order.wait()
                order.done(dve.scalar_tensor_tensor(out=acc_t[:, u, 0:D], in0=acc_t[:, u, 0:D],
                                                    scalar=den[:, 2:3], in1=exp_y[:, :],
                                                    op0=ALU.mult, op1=ALU.max))
                order.wait()
                dve.wait_ge(x_loaded[u], 16 * (turn + 1))
                order.done(dve.tensor_tensor(out=x1[:, u, :], in0=x1[:, u, :], in1=acc_t[:, u, 0:D],
                                             op=ALU.add))
                order.wait()
                for h in range(2):
                    last = dve.bn_stats(out=stats[:, 0, 6 * h:6 * h + 6],
                                        in_=x1[:, u, h * HALF:(h + 1) * HALF])
                order.done(last)
                order.wait()
                dve.sem_inc(S["stats_done"], 1)
                order.done(dve.bn_aggr(out=mean_var[:, 0, :], in_=stats[:, 0, :]))
                order.wait()
                dve.tensor_scalar(out=var_eps[:, :], in0=mean_var[:, :, 1], scalar1=EPS_LN, scalar2=None,
                                  op0=ALU.add).then_inc(S["var_ready"], 1)
                dve.wait_ge(S["rstd_ready"], t + (CH + 1))
                dve.tensor_copy(affine[:, 0:1], rstd[:, 0:1])
                dve.scalar_tensor_tensor(out=affine[:, 1:2], in0=mean_var[:, 0, 0:1], scalar=-1.0,
                                         in1=rstd[:, 0:1], op0=ALU.mult, op1=ALU.mult
                                         ).then_inc(S["norm_ready"], 1)

            def xnT(t):
                dve.wait_ge(S["xhi_n"], t + 1)
                dve.tensor_tensor(out=xnT_lo[:, :, :].rearrange("p k e -> p (k e)"), in0=tp[:, :],
                                  in1=xnT_hi[:, :, :].rearrange("p k e -> p (k e)").bitcast(f32),
                                  op=ALU.subtract).then_inc(S["xlo_n"], 1)

            def gT(t):
                dve.wait_ge(S["ghi_ready"], t + 1)
                dve.tensor_copy(wT[:, :], tp[0:KB, G:G + P])
                dve.tensor_tensor(out=gT_lo[:, :, :].rearrange("p k e -> p (k e)"), in0=tp[:, 0:G],
                                  in1=gT_hi[:, :, :].rearrange("p k e -> p (k e)").bitcast(f32),
                                  op=ALU.subtract).then_inc(S["glo_ready"], 1)

            def route(t):
                dve.wait_ge(S["gate_done"], t + 1)
                order.done(dve.tensor_tensor(out=lg[:, :], in0=pu[:, 2 * G:UP], in1=gb_bc[:, :], op=ALU.add))
                order.wait()
                dve.tensor_reduce(out=neg_max[:, :], in_=lg[:, :], axis=AX, op=ALU.max, negate=True
                                  ).then_inc(S["lmax_ready"], 1)
                mine = lg[:, :].unsqueeze(2).to_broadcast([P, NE, NE])
                other = lg[:, :].unsqueeze(1).to_broadcast([P, NE, NE])
                dve.tensor_tensor(out=greater[:, :, :], in0=other, in1=mine, op=ALU.is_gt)
                order.done(dve.tensor_tensor(out=equal[:, :, :], in0=other, in1=mine, op=ALU.is_equal))
                order.wait()
                order.done(dve.tensor_tensor(out=equal[:, :, :], in0=equal[:, :, :],
                                             in1=before[:, :, :], op=ALU.mult))
                order.wait()
                order.done(dve.tensor_tensor(out=greater[:, :, :], in0=greater[:, :, :],
                                             in1=equal[:, :, :], op=ALU.add))
                order.wait()
                order.done(dve.tensor_reduce(out=rank[:, :], in_=greater[:, :, :], axis=AX, op=ALU.add))
                dve.wait_ge(S["expl_ready"], t + 1)
                order.done(dve.reciprocal(exp_sum[:, 1:2], exp_sum[:, 0:1]))
                order.wait()
                order.done(dve.scalar_tensor_tensor(out=rank[:, :], in0=rank[:, :], scalar=1.5,
                                                    in1=exp_l[:, :], op0=ALU.is_lt, op1=ALU.mult))
                order.wait()
                order.done(dve.tensor_scalar(out=x_w[:, 0:NE], in0=rank[:, :], scalar1=exp_sum[:, 1:2],
                                             scalar2=0.5, op0=ALU.mult, op1=ALU.mult))
                order.wait()
                four = x_w_hl[:, :].rearrange("p (r c) -> p r c", r=2)
                w2 = x_w[:, :].unsqueeze(1).to_broadcast([P, 2, NX])
                order.done(dve.tensor_copy(four[:, :, 0:NX], w2))
                order.wait()
                order.done(dve.tensor_tensor(out=four[:, :, NX:2 * NX], in0=w2,
                                             in1=four[:, :, 0:NX].bitcast(f32), op=ALU.subtract))

            def glu_in(t):
                dve.wait_ge(S["up_done"], t + 1)
                dve.tensor_tensor(out=p1[:, :], in0=pu[:, 0:G], in1=b1_bc[:, :], op=ALU.add
                                  ).then_inc(S["p1_ready"], 1)
                dve.tensor_tensor(out=p2[:, :], in0=pu[:, G:2 * G], in1=b2_bc[:, :], op=ALU.add
                                  ).then_inc(S["pu_free"], 1)

            def glu(t):
                dve.wait_ge(S["th_ready"], t + 1)
                order.done(dve.scalar_tensor_tensor(out=p1[:, :], in0=th[:, :], scalar=1.0, in1=p1[:, :],
                                                    op0=ALU.add, op1=ALU.mult))
                order.wait()
                dve.wait_ge(S["pu_free"], t + 1)
                order.done(dve.tensor_tensor(out=p1[:, :], in0=p1[:, :], in1=p2[:, :], op=ALU.mult))
                order.wait()
                dve.tensor_tensor(out=p1[:, :].rearrange("p (e h) -> p e h", h=H),
                                  in0=p1[:, :].rearrange("p (e h) -> p e h", h=H),
                                  in1=x_w[:, :].unsqueeze(2).to_broadcast([P, NX, H]), op=ALU.mult
                                  ).then_inc(S["glu_ready"], 1)

            def output(t, u, turn):
                dve.wait_ge(S["d_done"], t + 1)
                dve.wait_ge(stored[u], 16 * turn)
                dve.tensor_tensor(out=out_t[:, u, :], in0=dp[:, :], in1=x1[:, u, :], op=ALU.add
                                  ).then_inc(S["out_ready"], 1)

            dve.wait_ge(S["acc_added"], 16 * CH)
            order.done(dve.memset(x_w_hl[:, :].bitcast(f32), 0.0))
            order.done(dve.memset(x_w[:, NE:NX], 0.5 / NS))
            order.wait()
            front(0, 0, 0)
            xnT(0)

            def dn_split(k):
                dve.wait_ge(S["dnhi_ready"], k + 1)
                dve.tensor_tensor(out=dn_lo[:, k, :], in0=out_t[:, k % 3, :],
                                  in1=dn_hi[:, k, :].bitcast(f32), op=ALU.subtract).then_inc(S["dn_ready"], 1)

            for k in range(3):
                dn_split(k)
            front(1, 1, 0)
            dve.wait_ge(S["const_ready"], 4)
            dve.wait_ge(S["consts_loaded"], 16 * 7)
            route(0)
            glu_in(0)
            xnT(1)
            glu(0)
            for k in range(3, KG):
                dn_split(k)
            dve.wait_ge(S["obhi_ready"], 1)
            dve.scalar_tensor_tensor(out=ob_hl[32:KB, :], in0=ob_raw[32:KB, :], scalar=2.0,
                                     in1=ob_hl[32:KB, :].bitcast(f32), op0=ALU.mult, op1=ALU.subtract
                                     ).then_inc(S["dn_ready"], 1)

            def step(t, u, turn):
                first = isinstance(t, int) and t == 1
                last = isinstance(t, int) and t == TL - 1
                if not last and first:
                    front(t + 1, (u + 1) % 3, turn + (u + 1) // 3)
                gT(t - 1)
                if not last and not first:
                    front(t + 1, (u + 1) % 3, turn + (u + 1) // 3)
                route(t)
                glu_in(t)
                glu(t)
                if not last:
                    xnT(t + 1)
                output(t - 1, (u - 1) % 3, turn + (u - 1) // 3)

            for t in range(1, 4):
                step(t, t % 3, t // 3)
            with dve.Fori(0, (TL - 7) // 3) as j:
                order.enter(j, 3 * NODE_STEPS)
                for v in range(4, 7):
                    step(j * 3 + v, v % 3, j + v // 3)
            order.leave((TL - 7) // 3)
            for t in range(TL - 3, TL):
                step(t, t % 3, t // 3)
            gT(TL - 1)
            output(TL - 1, (TL - 1) % 3, (TL - 1) // 3)

        @block.tensor
        def _(pe):
            def product(out_ap, hi, lo, w_hi_ap, w_lo_ap, start, end, first, last):
                pieces = [(c, min(c + HALF, end)) for c in range(start, end, HALF)]
                for left, right, s, e in ((hi, w_hi_ap, first, False), (hi, w_lo_ap, False, False),
                                          (lo, w_hi_ap, False, last)):
                    for c0, c1 in pieces:
                        mm = pe.matmul(out_ap[:, c0:c1], left, right[:, c0:c1], start=s, stop=e)
                return mm

            pe.wait_ge(S["const_ready"], 3)
            for k in range(KD):
                pe.wait_ge(S["vector_step"], DVE_SLICES[k])
                if k in POOL_K:
                    pe.wait_ge(S["u_part"], POOL_K.index(k) + 1)
                for l in range(2):
                    last = pe.matmul(hp[l][:, k * P:(k + 1) * P], u_col[:, l, k:k + 1].to_broadcast([P, P]),
                                     ident[:, :], start=True, stop=True)
            last.then_inc(S["u_ps"], 1)

            def aggregate(k, s):
                pe.wait_ge(S["split_ready"], k + 1)
                for d in range(KD):
                    for part in (x_hi, x_lo):
                        pe.matmul(agg[:, d * P:(d + 1) * P], part[:, d * P:(d + 1) * P], same[:, s, :],
                                  start=part is x_hi, stop=part is x_lo)
                pe.matmul(e_sum[:, 0:2], same[:, s, :], e_hl[:, :], start=True, stop=True
                          ).then_inc(S["agg_done"], 1)

            def times_w(k, s):
                pe.wait_ge(S["agglo_ready"], k + 1)
                pe.wait_ge(S["hp_free"], k + 1)
                for d in range(KD):
                    pe.wait_ge(S["w_split"], d + 1)
                    mm = product(hp[s], aggT_hi[:, s, d, :], aggT_lo[:, s, d, :], w_hi[:, d, :],
                                 w_lo[:, d, :], 0, D, d == 0, d == KD - 1)
                mm.then_inc(S["wmm_done"], 1)

            aggregate(0, 0)
            with pe.Fori(0, CH // 2) as j:
                for s in range(2):
                    aggregate(j * 2 + (s + 1), 1 - s)
                    times_w(j * 2 + s, s)
            times_w(CH - 1, 0)

            def transpose_xn(t):
                pe.wait_ge(S["xn_ready"], t + 1)
                if not isinstance(t, int) or t >= 2:
                    pe.wait_ge(S["glo_ready"], t - 1)
                for d in range(KD):
                    last = pe.transpose(tp[:, d * P:(d + 1) * P], xn[:, d * P:(d + 1) * P], ident[:, :])
                last.then_inc(S["t_done"], 1)

            def expert_up(t):
                pe.wait_ge(S["xlo_n"], t + 1)
                pe.wait_ge(S["pu_free"], t)
                for d in range(KD):
                    mm = product(pu, xnT_hi[:, d, :], xnT_lo[:, d, :], up_hi[:, d * UP:(d + 1) * UP],
                                 up_lo[:, d * UP:(d + 1) * UP], 2 * HALF, UP, d == 0, d == KD - 1)
                mm.then_inc(S["gate_done"], 1)
                for d in range(KD):
                    mm = product(pu, xnT_hi[:, d, :], xnT_lo[:, d, :], up_hi[:, d * UP:(d + 1) * UP],
                                 up_lo[:, d * UP:(d + 1) * UP], 0, 2 * HALF, d == 0, d == KD - 1)
                mm.then_inc(S["up_done"], 1)

            def transpose_glu(t):
                pe.wait_ge(S["glu_ready"], t + 1)
                if isinstance(t, int) and t == TL - 1:
                    pass
                else:
                    pe.wait_ge(S["xlo_n"], t + 2)
                for g in range(KG):
                    pe.transpose(tp[:, g * P:(g + 1) * P], p1[:, g * P:(g + 1) * P], ident[:, :])
                pe.transpose(tp[0:KB, G:G + P], x_w_hl[:, :].bitcast(f32), ident[:, :]
                             ).then_inc(S["v_done"], 1)

            def expert_down(t):
                pe.wait_ge(S["glo_ready"], t + 1)
                pe.wait_ge(S["out_ready"], t)
                for g in range(KG):
                    product(dp, gT_hi[:, g, :], gT_lo[:, g, :], dn_hi[:, g, :], dn_lo[:, g, :],
                            0, D, g == 0, False)
                for c in range(2):
                    mm = pe.matmul(dp[:, c * HALF:(c + 1) * HALF], wT[:, :],
                                   ob_hl[:, c * HALF:(c + 1) * HALF], start=False, stop=True)
                mm.then_inc(S["d_done"], 1)

            transpose_xn(0)
            expert_up(0)
            transpose_xn(1)
            expert_up(1)
            transpose_glu(0)
            transpose_xn(2)
            pe.wait_ge(S["dn_ready"], KG + 1)
            expert_down(0)
            transpose_glu(1)

            def step(t):
                expert_up(t)
                if not isinstance(t, int) or t < TL - 1:
                    transpose_xn(t + 1)
                expert_down(t - 1)
                transpose_glu(t)

            with pe.Fori(2, TL - 1) as t:
                step(t)
            step(TL - 1)
            expert_down(TL - 1)


def kernel(x, src, dst, L0_gnn_W, L0_gnn_a, L0_ffn_gate_w, L0_ffn_gate_b, L0_ffn_rw1, L0_ffn_rb1,
           L0_ffn_rw2, L0_ffn_rb2, L0_ffn_rw3, L0_ffn_rb3, L0_ffn_sw1, L0_ffn_sb1, L0_ffn_sw2,
           L0_ffn_sb2, L0_ffn_sw3, L0_ffn_sb3):
    import numpy as np
    import concourse.bacc as bacc
    from concourse.bass_utils import run_bass_kernel_spmd

    def columns(w1):
        return np.asarray(w1).transpose(1, 0, 2).reshape(D, -1)

    idx = np.zeros((CH * P, 4), np.int32)
    idx[:, 0] = N
    idx[:E, 0] = np.asarray(src)
    idx[:E, 1] = np.asarray(src)
    idx[:E, 2] = np.asarray(dst)
    idx[:, 3] = np.arange(CH * P)
    up = np.concatenate([columns(L0_ffn_rw1), columns(L0_ffn_sw1), columns(L0_ffn_rw2),
                         columns(L0_ffn_sw2), np.asarray(L0_ffn_gate_w)], axis=1)
    up = up.reshape(KD, P, UP).transpose(1, 0, 2).reshape(P, -1)
    up = np.concatenate([up, np.zeros((P, UPN * UPW - up.shape[1]), np.float32)], axis=1)
    ins = {
        "x": np.asarray(x), "idx": idx, "keys": idx[:, 0], "where0": np.full(N + 16, SKIP, np.int32),
        "w": np.asarray(L0_gnn_W), "a": np.asarray(L0_gnn_a),
        "up": up, "gate_b": np.asarray(L0_ffn_gate_b),
        "b1": np.concatenate([np.asarray(L0_ffn_rb1).ravel(), np.asarray(L0_ffn_sb1).ravel()]),
        "b2": np.concatenate([np.asarray(L0_ffn_rb2).ravel(), np.asarray(L0_ffn_sb2).ravel()]),
        "dn": np.concatenate([np.asarray(L0_ffn_rw3).reshape(-1, D), np.asarray(L0_ffn_sw3).reshape(-1, D)]),
        "ob": np.concatenate([np.asarray(L0_ffn_rb3), np.asarray(L0_ffn_sb3)]),
    }
    nc = bacc.Bacc("TRN2", target_bir_lowering=False, num_devices=1)
    arrays, aps = {}, []
    for name, value in ins.items():
        value = np.ascontiguousarray(value)
        arrays[f"in_{name}"] = value
        aps.append(nc.dram_tensor(f"in_{name}", value.shape, mybir.dt.from_np(value.dtype),
                                  kind="ExternalInput").ap())
    aps.append(nc.dram_tensor("out_0", (N, D), mybir.dt.float32, kind="ExternalOutput").ap())
    build(nc, *aps)
    return run_bass_kernel_spmd(nc, [arrays], core_ids=[0]).results[0]["out_0"]
```
